# Optimizing a Trainium2 kernel written in Bass

```python
import numpy as np
import jax
import jax.numpy as jnp

def _softmax(x, axis=-1):
    return jax.nn.softmax(x, axis=axis)

def _gelu(x):
    return jax.nn.gelu(x, approximate=True)

def _silu(x):
    return jax.nn.silu(x)

def _sigmoid(x):
    return jax.nn.sigmoid(x)

def _layernorm(x, axis=-1, eps=1e-05):
    m = jnp.mean(x, axis=axis, keepdims=True)
    v = jnp.var(x, axis=axis, keepdims=True)
    return (x - m) / jnp.sqrt(v + eps)

def _scatter_add(tgt, idx, src, axis=0):
    return tgt.at[idx].add(src)

def _segment_sum(src, seg, n):
    return jax.ops.segment_sum(src, seg, n)
kernel_name = 'mk_adj_ffn_d2_adj_r2_bd3692'

def setup_inputs(seed: int=0):
    np.random.seed(seed)
    _w = jnp.asarray

    def _rec_inputs():
        import jax
        import jax.numpy as jnp
        _gk = jax.random.key(seed)
        x = -0.0003929 + 0.9999 * jax.random.normal(jax.random.fold_in(_gk, 1), (128, 64, 128), jnp.float32)
        _a = jax.random.bernoulli(jax.random.fold_in(_gk, 2), 0.0625, (64, 64))
        _a = jnp.logical_or(_a, jnp.swapaxes(_a, -1, -2))
        _a = jnp.logical_or(_a, jnp.eye(64, dtype=bool))
        _af = _a.astype(jnp.float32)
        _d = jnp.maximum(_af.sum(-1), 1.0) ** (-0.5)
        _af = _af * _d[..., :, None] * _d[..., None, :]
        adj = _af
        return (x, adj)
    x, adj = _rec_inputs()

    def _L0_gnn_setup():
        import jax, jax.numpy as jnp
        import numpy as np
        B, N, D_IN, HID, D_OUT = (64, 512, 128, 128, 128)
        key = jax.random.key(seed)
        kf, ka, kw1, kw2 = jax.random.split(key, 4)
        features = jax.random.normal(kf, (B, N, D_IN), dtype=jnp.float32)
        A = jax.random.uniform(ka, (N, N), dtype=jnp.float32)
        A = 0.5 * (A + A.T)
        lim1 = float(np.sqrt(6.0 / (D_IN + HID)))
        lim2 = float(np.sqrt(6.0 / (HID + D_OUT)))
        W1 = jax.random.uniform(kw1, (D_IN, HID), minval=-lim1, maxval=lim1, dtype=jnp.float32)
        b1 = jnp.zeros((HID,), jnp.float32)
        W2 = jax.random.uniform(kw2, (HID, D_OUT), minval=-lim2, maxval=lim2, dtype=jnp.float32)
        b2 = jnp.zeros((D_OUT,), jnp.float32)
        return {'features': features, 'A': A, 'W1': W1, 'b1': b1, 'W2': W2, 'b2': b2}
    _L0_gnn_all = _L0_gnn_setup()
    _L0_gnn_in = {k: v for k, v in _L0_gnn_all.items() if k in ('W1', 'b1', 'W2', 'b2')}
    del _L0_gnn_all

    def _L0_ffn_setup():
        import jax, jax.numpy as jnp
        import numpy as np
        N_EXPERTS = 8
        TOP_K = 2
        key = jax.random.key(seed)
        ks = jax.random.split(key, 5)
        B, T, C, E, H = (8, 1024, 128, 8, 341)
        scale = 1.0 / np.sqrt(C)
        return {'x': jax.random.normal(ks[0], (B, T, C), dtype=jnp.float32), 'router_w': jax.random.normal(ks[1], (E, C), dtype=jnp.float32) * scale, 'w1': jax.random.normal(ks[2], (E, H, C), dtype=jnp.float32) * scale, 'w2': jax.random.normal(ks[3], (E, C, H), dtype=jnp.float32) * (1.0 / np.sqrt(H)), 'w3': jax.random.normal(ks[4], (E, H, C), dtype=jnp.float32) * scale}
    _L0_ffn_all = _L0_ffn_setup()
    _L0_ffn_in = {k: v for k, v in _L0_ffn_all.items() if k in ('router_w', 'w1', 'w2', 'w3')}
    del _L0_ffn_all

    def _L1_gnn_setup():
        import jax, jax.numpy as jnp
        import numpy as np
        EPS = 1e-05

        def _batchnorm(x, gamma, beta):
            mu = jnp.mean(x, axis=0)
            var = jnp.var(x, axis=0)
            return (x - mu) * jax.lax.rsqrt(var + EPS) * gamma + beta
        key = jax.random.key(seed)
        ks = jax.random.split(key, 4)
        b, n, d, h, o = (32, 1024, 128, 256, 128)
        features = jax.random.normal(ks[0], (b, n, d), dtype=jnp.float32)
        A = jax.random.uniform(ks[1], (n, n), dtype=jnp.float32)
        lim1 = float(np.sqrt(6.0 / (d + h)))
        W1 = jax.random.uniform(ks[2], (h, d), minval=-lim1, maxval=lim1, dtype=jnp.float32)
        b1 = jnp.zeros((h,), jnp.float32)
        lim2 = float(np.sqrt(6.0 / (h + o)))
        W2 = jax.random.uniform(ks[3], (o, h), minval=-lim2, maxval=lim2, dtype=jnp.float32)
        b2 = jnp.zeros((o,), jnp.float32)
        g1 = jnp.ones((h,), jnp.float32)
        be1 = jnp.zeros((h,), jnp.float32)
        g2 = jnp.ones((o,), jnp.float32)
        be2 = jnp.zeros((o,), jnp.float32)
        return {'features': features, 'A': A, 'W1': W1, 'b1': b1, 'g1': g1, 'be1': be1, 'W2': W2, 'b2': b2, 'g2': g2, 'be2': be2}
    _L1_gnn_all = _L1_gnn_setup()
    _L1_gnn_in = {k: v for k, v in _L1_gnn_all.items() if k in ('W1', 'b1', 'g1', 'be1', 'W2', 'b2', 'g2', 'be2')}
    del _L1_gnn_all

    def _L1_ffn_setup():
        import jax, jax.numpy as jnp
        import numpy as np
        B, S, D, F, E, K = (8, 1024, 128, 512, 8, 2)
        key = jax.random.key(seed)
        ks = jax.random.split(key, 10)
        s = 0.02
        return {'x': jax.random.normal(ks[0], (B, S, D), dtype=jnp.float32), 'Wr': jax.random.normal(ks[1], (D, E), dtype=jnp.float32) * s, 'W1s': jax.random.normal(ks[2], (D, F), dtype=jnp.float32) * s, 'b1s': jnp.zeros((F,), dtype=jnp.float32), 'W2s': jax.random.normal(ks[3], (F, D), dtype=jnp.float32) * s, 'b2s': jnp.zeros((D,), dtype=jnp.float32), 'W1p': jax.random.normal(ks[4], (E, D, F), dtype=jnp.float32) * s, 'b1p': jnp.zeros((E, F), dtype=jnp.float32), 'W2p': jax.random.normal(ks[5], (E, F, D), dtype=jnp.float32) * s, 'b2p': jnp.zeros((E, D), dtype=jnp.float32)}
    _L1_ffn_all = _L1_ffn_setup()
    _L1_ffn_in = {k: v for k, v in _L1_ffn_all.items() if k in ('Wr', 'W1s', 'b1s', 'W2s', 'b2s', 'W1p', 'b1p', 'W2p', 'b2p')}
    del _L1_ffn_all
    return {'x': x, 'adj': adj, 'L0_gnn_W1': _L0_gnn_in['W1'], 'L0_gnn_b1': _L0_gnn_in['b1'], 'L0_gnn_W2': _L0_gnn_in['W2'], 'L0_gnn_b2': _L0_gnn_in['b2'], 'L0_ffn_router_w': _L0_ffn_in['router_w'], 'L0_ffn_w1': _L0_ffn_in['w1'], 'L0_ffn_w2': _L0_ffn_in['w2'], 'L0_ffn_w3': _L0_ffn_in['w3'], 'L1_gnn_W1': _L1_gnn_in['W1'], 'L1_gnn_b1': _L1_gnn_in['b1'], 'L1_gnn_g1': _L1_gnn_in['g1'], 'L1_gnn_be1': _L1_gnn_in['be1'], 'L1_gnn_W2': _L1_gnn_in['W2'], 'L1_gnn_b2': _L1_gnn_in['b2'], 'L1_gnn_g2': _L1_gnn_in['g2'], 'L1_gnn_be2': _L1_gnn_in['be2'], 'L1_ffn_Wr': _L1_ffn_in['Wr'], 'L1_ffn_W1s': _L1_ffn_in['W1s'], 'L1_ffn_b1s': _L1_ffn_in['b1s'], 'L1_ffn_W2s': _L1_ffn_in['W2s'], 'L1_ffn_b2s': _L1_ffn_in['b2s'], 'L1_ffn_W1p': _L1_ffn_in['W1p'], 'L1_ffn_b1p': _L1_ffn_in['b1p'], 'L1_ffn_W2p': _L1_ffn_in['W2p'], 'L1_ffn_b2p': _L1_ffn_in['b2p']}

def reference(x, adj, L0_gnn_W1, L0_gnn_b1, L0_gnn_W2, L0_gnn_b2, L0_ffn_router_w, L0_ffn_w1, L0_ffn_w2, L0_ffn_w3, L1_gnn_W1, L1_gnn_b1, L1_gnn_g1, L1_gnn_be1, L1_gnn_W2, L1_gnn_b2, L1_gnn_g2, L1_gnn_be2, L1_ffn_Wr, L1_ffn_W1s, L1_ffn_b1s, L1_ffn_W2s, L1_ffn_b2s, L1_ffn_W1p, L1_ffn_b1p, L1_ffn_W2p, L1_ffn_b2p):
    import jax
    import jax.numpy as jnp

    def _L0_gnn_ref(features, A, W1, b1, W2, b2):
        import jax, jax.numpy as jnp
        import numpy as np
        B, N, D_IN, HID, D_OUT = (64, 512, 128, 128, 128)
        deg = jnp.sum(A, axis=0) + jnp.sum(A, axis=1) - jnp.diagonal(A)
        d_inv_sqrt = jnp.where(deg > 0, jax.lax.rsqrt(deg), 0.0)
        L = jnp.diag(deg) - A
        L_norm = d_inv_sqrt[:, None] * L * d_inv_sqrt[None, :]
        _, U = jnp.linalg.eigh(L_norm)
        agg = jnp.einsum('mn,bnd->bmd', U.T, features)
        h = jax.nn.relu(agg @ W1 + b1)
        out = h @ W2 + b2
        return jnp.einsum('nm,bmd->bnd', U, out)

    def _L0_ffn_ref(x, router_w, w1, w2, w3):
        import jax, jax.numpy as jnp
        import numpy as np
        N_EXPERTS = 8
        TOP_K = 2
        B, T, C = x.shape
        flat = x.reshape(-1, C)
        logits = flat @ router_w.T
        probs = jax.nn.softmax(logits, axis=-1)
        topk_probs, topk_idx = jax.lax.top_k(probs, TOP_K)
        topk_probs = topk_probs / (jnp.sum(topk_probs, axis=-1, keepdims=True) + 1e-09)
        onehot = jax.nn.one_hot(topk_idx, N_EXPERTS, dtype=flat.dtype)
        gates = jnp.einsum('nk,nke->ne', topk_probs, onehot)
        h1 = jnp.einsum('nc,ehc->neh', flat, w1)
        h3 = jnp.einsum('nc,ehc->neh', flat, w3)
        h = jax.nn.silu(h1) * h3
        y = jnp.einsum('neh,ech->nec', h, w2)
        out = jnp.einsum('ne,nec->nc', gates, y)
        return out.reshape(B, T, C)

    def _L1_gnn_ref(features, A, W1, b1, g1, be1, W2, b2, g2, be2):
        import jax, jax.numpy as jnp
        import numpy as np
        EPS = 1e-05

        def _batchnorm(x, gamma, beta):
            mu = jnp.mean(x, axis=0)
            var = jnp.var(x, axis=0)
            return (x - mu) * jax.lax.rsqrt(var + EPS) * gamma + beta
        b, n, d = features.shape
        A_norm = A + jnp.eye(n, dtype=A.dtype)
        deg = jnp.sum(A_norm, axis=0) + jnp.sum(A_norm, axis=1) - jnp.diagonal(A_norm)
        dinv = jax.lax.rsqrt(deg)
        A_hat = A_norm * dinv[:, None] * dinv[None, :]
        agg = jnp.einsum('nm,bmd->bnd', A_hat, features)
        x = agg.reshape(-1, d)
        h = jax.nn.relu(_batchnorm(x @ W1.T + b1, g1, be1))
        out = h @ W2.T + b2
        out = _batchnorm(out, g2, be2)
        return out.reshape(b, n, -1)

    def _L1_ffn_ref(x, Wr, W1s, b1s, W2s, b2s, W1p, b1p, W2p, b2p):
        import jax, jax.numpy as jnp
        import numpy as np
        B, S, D, F, E, K = (8, 1024, 128, 512, 8, 2)
        gelu = lambda t: jax.nn.gelu(t, approximate=False)
        shared = gelu(x @ W1s + b1s) @ W2s + b2s
        rw = jax.nn.softmax(x @ Wr, axis=-1)
        topw, topi = jax.lax.top_k(rw, K)
        topw = topw / jnp.sum(topw, axis=-1, keepdims=True)
        mask = jnp.sum(jax.nn.one_hot(topi, E, dtype=topw.dtype) * topw[..., None], axis=-2)
        h = gelu(jnp.einsum('bsd,edf->bsef', x, W1p) + b1p)
        priv = jnp.einsum('bsef,efd->bsed', h, W2p) + b2p
        routed = jnp.einsum('bsed,bse->bsd', priv, mask)
        return shared + routed
    x = x + _L0_gnn_ref(_layernorm(x, axis=-1), adj, L0_gnn_W1, L0_gnn_b1, L0_gnn_W2, L0_gnn_b2)
    x = x + _L0_ffn_ref(_layernorm(x, axis=-1), L0_ffn_router_w, L0_ffn_w1, L0_ffn_w2, L0_ffn_w3)
    x = x + _L1_gnn_ref(_layernorm(x, axis=-1), adj, L1_gnn_W1, L1_gnn_b1, L1_gnn_g1, L1_gnn_be1, L1_gnn_W2, L1_gnn_b2, L1_gnn_g2, L1_gnn_be2)
    x = x + _L1_ffn_ref(_layernorm(x, axis=-1), L1_ffn_Wr, L1_ffn_W1s, L1_ffn_b1s, L1_ffn_W2s, L1_ffn_b2s, L1_ffn_W1p, L1_ffn_b1p, L1_ffn_W2p, L1_ffn_b2p)
    return x

_drawn_inputs = setup_inputs


def setup_inputs(seed=0):
    import zlib

    import numpy as np

    out = dict(_drawn_inputs(seed))
    spreads = {'L0_gnn_b1': (0.0, 0.1),
     'L0_gnn_b2': (0.0, 0.1),
     'L1_gnn_b1': (0.0, 0.8),
     'L1_gnn_g1': (1.0, 0.2),
     'L1_gnn_be1': (0.0, 0.1),
     'L1_gnn_b2': (0.0, 0.8),
     'L1_gnn_g2': (1.0, 0.2),
     'L1_gnn_be2': (0.0, 0.1),
     'L1_ffn_b1s': (0.0, 0.583),
     'L1_ffn_b2s': (0.0, 0.1),
     'L1_ffn_b1p': (0.0, 0.763),
     'L1_ffn_b2p': (0.0, 0.1)}
    factors = {}
    for name, (base, spread) in spreads.items():
        noise = np.random.default_rng([zlib.crc32(name.encode()), seed]).standard_normal(out[name].shape)
        drawn = base * np.exp(spread * noise) if base else spread * noise
        out[name] = jnp.asarray(drawn.astype(out[name].dtype))
    for name, factor in factors.items():
        out[name] = (out[name] * factor).astype(out[name].dtype)
    return out
```

```python
import numpy as np
import concourse.bass as bass
from concourse import mybir
from contextlib import ExitStack

F32 = mybir.dt.float32
ALU = mybir.AluOpType
ACT = mybir.ActivationFunctionType
AX = mybir.AxisListType

N = 64
P = 128
D = 128
STEPS = N - 2
POINTS = 8
PASSES = 7
REFINE = 3
BIG = 1e15

C_ID = 0
C_ONE = C_ID + P
C_LOW = C_ONE + P
C_SEL = C_LOW + N
C_DUP = C_SEL + N
C_PT = C_DUP + P
C_DOWN = C_PT + POINTS
C_J = C_DOWN + N
C_EXP = C_J + 1
C_COLS = C_EXP + 32


def constants():
    c = np.zeros((P, C_COLS), np.float32)
    i = np.arange(P)
    c[:, C_ID:C_ID + P] = np.eye(P)
    c[:, C_ONE:C_ONE + P] = 1
    c[:N, C_LOW:C_LOW + N] = i[:N, None] > i[None, :N]
    c[:N, C_SEL:C_SEL + N] = i[:N, None] == i[None, :N] + 1
    c[:N, C_DUP:C_DUP + P] = i[:N, None] == i[None, :] % N
    c[:, C_PT:C_PT + POINTS] = np.arange(1, POINTS + 1)
    c[:, C_DOWN:C_DOWN + N] = N - np.arange(N)
    c[:, C_J] = i % N
    c[:, C_EXP:C_EXP + 32] = np.tile(8 - np.arange(8), 4)
    return c


class Count:

    def __init__(self, eng, sem):
        self.eng, self.sem, self.n = eng, sem, 0

    def inc(self, ins):
        self.n += 1
        ins.then_inc(self.sem, 1)
        return self.n

    def chain(self, ins):
        self.eng.wait_ge(self.sem, self.inc(ins))
        return self.n


def hold(eng, sem, value):
    eng.wait_ge(sem, value)
    eng.nop(nofuse=True)


def eig_memory(sb, pb):
    m = {}
    for name, shape in dict(
        A=[N, N], AT=[P, N], rowsum=[P, 4], dinv=[P, 4], dd=[P, N], L=[N, N], LT=[N, N],
        Ah=[P, N], tri=[N, N], QT=[N, N], Q=[N, N], X3=[N, 3], S2=[N, 3], c=[N, 8], v=[N, 1],
        rowv=[1, N], rowu=[1, N], H=[N, N], B=[N, N], AI=[N, 2 * N],
        TB=[P, N], EB=[P, N], NE2=[P, N], lim=[P, 8], xs=[P, POINTS],
        TX=[P, N * POINTS], PV=[P, N * POINTS], RC=[P, POINTS], neg=[P, N * POINTS], cnt=[P, POINTS],
        PVC=[P, N], DM=[N, N], g=[N, N], g2=[N, N], onehot=[N, N], rf=[N, N], rb=[N, N], zf=[N, N], zb=[N, N],
        Z=[N, N], ZT=[N, N], sq=[N, N], zc=[N, 8],
        X=[N, N], XT=[N, N], R=[N, N], AX=[N, N], LD=[N, N], den=[N, N], num=[N, N], E0=[N, N], mask=[N, N],
        W=[N, N], sg=[N, 8], sc=[N, 24], UT2=[N, P],
    ).items():
        m[name] = sb("eg_" + name, shape)
    return m


def eig_vector(nc, dve, S, C, m, ps, k1, k2, UB, UTB, AHB):
    V = nc.vector
    own = Count(dve, S("eig_dve"))
    ch = own.chain
    ident = C[0:N, C_ID:C_ID + N]
    low = C[0:N, C_LOW:C_LOW + N]
    sel = C[0:N, C_SEL:C_SEL + N]
    A, AT = m["A"], m["AT"]
    dve.wait_ge(S("const_in"), 16)
    dve.wait_ge(S("adj_in"), 48)
    rs, dinv = m["rowsum"], m["dinv"]
    V.tensor_reduce(rs[0:N, 0:1], A[:, :], AX.X, ALU.add).then_inc(own.sem, 1); own.n += 1
    V.tensor_reduce(rs[0:N, 1:2], AT[0:N, :], AX.X, ALU.add).then_inc(own.sem, 1); own.n += 1
    ch(V.tensor_tensor(m["sq"][:, :], A[:, :], ident, ALU.mult))
    ch(V.tensor_reduce(rs[0:N, 2:3], m["sq"][:, :], AX.X, ALU.add))
    ch(V.tensor_tensor(rs[0:N, 3:4], rs[0:N, 0:1], rs[0:N, 1:2], ALU.add))
    ch(V.tensor_tensor(dinv[0:N, 0:1], rs[0:N, 3:4], rs[0:N, 2:3], ALU.subtract))
    ch(V.tensor_scalar(dinv[0:N, 1:2], dinv[0:N, 0:1], 1.0, None, ALU.add))
    V.tensor_scalar(dinv[0:N, 3:4], dinv[0:N, 0:1], 0.0, None, ALU.is_gt).then_inc(own.sem, 1); own.n += 1
    ch(V.tensor_scalar(dinv[0:N, 2:3], dinv[0:N, 0:1], 1e-30, None, ALU.max))
    V.tensor_copy(m["c"][:, 0:1], dinv[0:N, 2:3]).then_inc(own.sem, 1); own.n += 1
    V.tensor_copy(m["c"][:, 1:2], dinv[0:N, 1:2]).then_inc(S("deg_ready"), 1)
    dve.wait_ge(S("deg_root"), 1)
    ch(V.reciprocal(m["c"][:, 4:6], m["c"][:, 2:4]))
    ch(V.tensor_tensor(m["c"][:, 4:5], m["c"][:, 4:5], dinv[0:N, 3:4], ALU.mult))
    ch(V.tensor_scalar(m["AI"][:, 0:N], ident, m["c"][:, 4:5], None, ALU.mult))
    V.tensor_scalar(m["AI"][:, N:2 * N], ident, m["c"][:, 5:6], None, ALU.mult).then_inc(S("dinv_diag"), 1)
    ch(V.tensor_scalar(m["L"][:, :], ident, dinv[0:N, 0:1], None, ALU.mult))
    ch(V.tensor_tensor(m["L"][:, :], m["L"][:, :], A[:, :], ALU.subtract))
    ch(V.tensor_scalar(m["L"][:, :], m["L"][:, :], m["c"][:, 4:5], None, ALU.mult))
    dve.wait_ge(S("dinv_rows"), 1)
    ch(V.tensor_tensor(m["L"][:, :], m["L"][:, :], ps[0][0:N, 0:N], ALU.mult))
    V.tensor_copy(m["dd"][:, 0:1], ps[0][:, P:P + 1]).then_inc(own.sem, 1); own.n += 1
    ch(V.tensor_tensor(m["Ah"][0:N, :], AT[0:N, :], ident, ALU.add))
    ch(V.tensor_tensor(m["Ah"][N:P, :], AT[N:P, :], C[N:P, C_ID + N:C_ID + P], ALU.add))
    ch(V.tensor_scalar(m["Ah"][:, :], m["Ah"][:, :], m["dd"][:, 0:1], None, ALU.mult))
    ch(V.memset(AHB[:, :], 0.0))
    ch(V.memset(UB[:, :], 0.0))
    ch(V.memset(UTB[:, :], 0.0))
    for h in (0, N):
        ch(V.tensor_tensor(AHB[h:h + N, h:h + N], m["Ah"][h:h + N, :], ps[0][h:h + N, N:2 * N], ALU.mult))
    V.tensor_copy(m["QT"][:, :], ident).then_inc(own.sem, 1); own.n += 1
    V.nop() if False else None
    dve.wait_ge(S("eig_dve"), own.n)
    V.tensor_copy(m["H"][:, :], m["L"][:, :]).then_inc(S("lap_ready"), 1)
    dve.wait_ge(S("lap_turned"), 1)
    ch(V.tensor_tensor(m["L"][:, :], m["L"][:, :], ps[1][0:N, 0:N], ALU.add))
    V.tensor_scalar(m["L"][:, :], m["L"][:, :], 0.5, None, ALU.mult).then_inc(S("lap_sym"), 1)

    hd, hp, ha = S("hh_dve"), S("hh_pe"), S("hh_act")
    ND, NP, NA = 17, 6, 2
    psA, psN, psR, psH, psB = ps[0], ps[1], ps[2], ps[3], ps[4]
    X3, S2, c = m["X3"], m["S2"], m["c"]
    with dve.Fori(0, STEPS) as k:
        b = k * ND

        def step(n, ins, wait=True):
            ins.then_inc(hd, 1)
            if wait:
                hold(dve, hd, b + n)
        hold(dve, hp, k * NP + 1)
        step(1, V.tensor_copy(X3[:, 1:2], sel[:, bass.ds(k, 1)]), False)
        step(2, V.tensor_tensor(X3[:, 2:3], psA[0:N, bass.ds(k, 1)], low[:, bass.ds(k + 1, 1)], ALU.mult), False)
        step(3, V.tensor_tensor(X3[:, 0:1], psA[0:N, bass.ds(k, 1)], low[:, bass.ds(k, 1)], ALU.mult), False)
        hold(dve, hp, k * NP + 2)
        step(4, V.tensor_copy(S2[:, :], psN[0:N, 0:3]), False)
        step(5, V.tensor_scalar(c[:, 0:1], psN[0:N, 1:2], 0.0, 2.0, ALU.is_ge, ALU.mult), False)
        step(6, V.tensor_scalar(c[:, 1:2], psN[0:N, 2:3], 0.0, None, ALU.is_gt))
        hold(dve, ha, k * NA + 1)
        step(7, V.scalar_tensor_tensor(out=c[:, 2:3], in0=c[:, 0:1], scalar=-1.0, in1=c[:, 7:8],
                                       op0=ALU.add, op1=ALU.mult))
        step(8, V.scalar_tensor_tensor(out=m["v"][:, :], in0=X3[:, 1:2], scalar=c[:, 2:3], in1=X3[:, 0:1],
                                       op0=ALU.mult, op1=ALU.add), False)
        step(9, V.scalar_tensor_tensor(out=c[:, 3:4], in0=S2[:, 1:2], scalar=c[:, 2:3], in1=S2[:, 0:1],
                                       op0=ALU.mult, op1=ALU.add))
        step(10, V.tensor_scalar(c[:, 3:4], c[:, 3:4], 1e-36, None, ALU.max))
        step(11, V.reciprocal(c[:, 4:5], c[:, 3:4]))
        step(12, V.tensor_tensor(c[:, 5:6], c[:, 4:5], c[:, 1:2], ALU.mult))
        hold(dve, hp, k * NP + 3)
        step(13, V.tensor_copy(m["rowv"][:, :], psR[0:1, 0:N]), False)
        step(14, V.tensor_scalar(m["rowu"][:, :], psR[0:1, 0:N], c[0:1, 5:6], None, ALU.mult), False)
        hold(dve, hp, k * NP + 4)
        step(15, V.tensor_tensor(m["H"][:, :], ident, psH[0:N, 0:N], ALU.subtract), False)
        hold(dve, hp, k * NP + 5)
        step(16, V.tensor_copy(m["B"][:, :], psB[0:N, 0:N]), False)
        hold(dve, hp, k * NP + 7)
        step(17, V.tensor_copy(m["QT"][:, :], ps[5][0:N, 0:N]), False)

    ch(V.tensor_tensor(m["AI"][:, 0:N], psA[0:N, 0:N], ident, ALU.mult))
    V.tensor_tensor(m["AI"][:, N:2 * N], psA[0:N, 0:N], sel, ALU.mult).then_inc(S("tri_parts"), 1)
    TB, EB, NE2, lim = m["TB"], m["EB"], m["NE2"], m["lim"]
    ch(V.memset(EB[:, :], 0.0))
    dve.wait_ge(S("tri_rows"), 1)
    ch(V.tensor_copy(TB[0:N, :], ps[1][0:N, 0:N]))
    ch(V.tensor_copy(TB[N:P, :], ps[1][N:P, 0:N][:, ::-1]))
    ch(V.tensor_copy(EB[0:N, 0:N - 1], ps[1][0:N, N:2 * N - 1]))
    ch(V.tensor_copy(EB[N:P, 0:N - 1], ps[1][N:P, N:2 * N - 1][:, ::-1]))
    ch(V.tensor_tensor(NE2[:, :], EB[:, :], EB[:, :], ALU.mult))
    ch(V.tensor_scalar(NE2[:, :], NE2[:, :], 1e-30, -1.0, ALU.max, ALU.mult))
    ch(V.tensor_reduce(lim[:, 0:1], TB[:, :], AX.X, ALU.max, apply_absolute_value=True))
    ch(V.tensor_reduce(lim[:, 1:2], EB[:, :], AX.X, ALU.max, apply_absolute_value=True))
    ch(V.scalar_tensor_tensor(out=lim[:, 2:3], in0=lim[:, 1:2], scalar=2.0, in1=lim[:, 0:1],
                              op0=ALU.mult, op1=ALU.add))
    ch(V.tensor_scalar(lim[:, 2:3], lim[:, 2:3], 1.001, 1e-20, ALU.mult, ALU.add))
    ch(V.tensor_scalar(lim[:, 3:4], lim[:, 2:3], -1.0, None, ALU.mult))
    ch(V.tensor_scalar(lim[:, 4:5], lim[:, 2:3], 2.0 / (POINTS + 1), None, ALU.mult))

    TX = m["TX"][:, :].rearrange("p (i q) -> p i q", i=N)
    PV = m["PV"][:, :].rearrange("p (i q) -> p i q", i=N)
    RC = m["RC"]

    def pivots(link, q):
        link(V.tensor_tensor(TX[:, :, 0:q], TB[:, :].unsqueeze(2).to_broadcast([P, N, q]),
                             m["xs"][:, 0:q].unsqueeze(1).to_broadcast([P, N, q]), ALU.subtract))
        link(V.tensor_copy(PV[:, 0, 0:q], TX[:, 0, 0:q]))
        for i in range(1, N):
            link(V.reciprocal(RC[:, 0:q], PV[:, i - 1, 0:q]))
            link(V.scalar_tensor_tensor(out=PV[:, i, 0:q], in0=RC[:, 0:q], scalar=NE2[:, i - 1:i],
                                        in1=TX[:, i, 0:q], op0=ALU.mult, op1=ALU.add))

    sect = S("sect_dve")
    PER = 2 + 2 * (N - 1) + 6
    with dve.Fori(0, PASSES) as p:
        at = [0]

        def link(ins):
            at[0] += 1
            ins.then_inc(sect, 1)
            hold(dve, sect, p * PER + at[0])
        link(V.tensor_scalar(m["xs"][:, :], C[:, C_PT:C_PT + POINTS], lim[:, 4:5], lim[:, 3:4], ALU.mult, ALU.add))
        pivots(link, POINTS)
        link(V.tensor_scalar(m["neg"][:, :], m["PV"][:, :], 0.0, None, ALU.is_lt))
        link(V.tensor_reduce(m["cnt"][:, :], m["neg"][:, :].rearrange("p (i q) -> p q i", i=N), AX.X, ALU.add))
        link(V.tensor_scalar(RC[:, :], m["cnt"][:, :], C[:, C_J:C_J + 1], None, ALU.is_le, ALU.add,
                             accum_out=lim[:, 5:6]))
        link(V.scalar_tensor_tensor(out=lim[:, 3:4], in0=lim[:, 5:6], scalar=lim[:, 4:5], in1=lim[:, 3:4],
                                    op0=ALU.mult, op1=ALU.add))
        link(V.tensor_scalar(lim[:, 4:5], lim[:, 4:5], 1.0 / (POINTS + 1), None, ALU.mult))
        assert at[0] == PER, at
    ch(V.scalar_tensor_tensor(out=lim[:, 6:7], in0=lim[:, 4:5], scalar=0.5 * (POINTS + 1), in1=lim[:, 3:4],
                              op0=ALU.mult, op1=ALU.add))
    V.tensor_copy(lim[:, 7:8], lim[:, 6:7]).then_inc(S("lam_ready"), 1)
    dve.wait_ge(S("lam_both"), 1)
    ch(V.tensor_copy(m["xs"][:, 0:1], ps[2][:, 0:1]))
    pivots(ch, 1)
    ch(V.tensor_scalar(m["PVC"][:, :], PV[:, :, 0], BIG, -BIG, ALU.min, ALU.max))
    V.tensor_copy(m["PVC"][:, 0:1], m["PVC"][:, 0:1]).then_inc(S("pivots_ready"), 1)
    dve.wait_ge(S("pivots_moved"), 1)
    DF, DM = m["PVC"][0:N, :], m["DM"]
    ch(V.tensor_copy(DM[:, :], ps[3][0:N, 0:N][:, ::-1]))
    g, g2, oh = m["g"], m["g2"], m["onehot"]
    ch(V.tensor_tensor(g[:, :], DM[:, :], DF, ALU.add))
    ch(V.tensor_tensor(g[:, :], g[:, :], TX[0:N, :, 0], ALU.subtract))
    ch(V.tensor_tensor(g[:, :], g[:, :], g[:, :], ALU.mult))
    ch(V.tensor_reduce(m["zc"][:, 0:1], g[:, :], AX.X, ALU.min))
    ch(V.scalar_tensor_tensor(out=g2[:, :], in0=g[:, :], scalar=m["zc"][:, 0:1], in1=C[0:N, C_DOWN:C_DOWN + N],
                              op0=ALU.is_le, op1=ALU.mult))
    ch(V.tensor_reduce(m["zc"][:, 1:2], g2[:, :], AX.X, ALU.max))
    ch(V.tensor_scalar(oh[:, :], g2[:, :], m["zc"][:, 1:2], None, ALU.is_equal))
    for r, d in ((m["rf"], DF), (m["rb"], DM[:, :])):
        ch(V.reciprocal(r[:, :], d))
        ch(V.tensor_scalar(r[:, :], r[:, :], 1e18, -1e18, ALU.min, ALU.max))
        ch(V.tensor_scalar(r[:, :], r[:, :], -1.0, None, ALU.mult))
    ch(V.tensor_tensor(m["rf"][:, 0:N], m["rf"][:, 0:N], EB[0:N, 0:N], ALU.mult))
    ch(V.tensor_tensor(m["rb"][:, 1:N], m["rb"][:, 1:N], EB[0:N, 0:N - 1], ALU.mult))
    ch(V.memset(m["rb"][:, 0:1], 0.0))
    ch(V.tensor_tensor_scan(m["zf"][:, :], m["rb"][:, :], oh[:, :], 0.0, ALU.mult, ALU.add))
    ch(V.tensor_tensor_scan(m["zb"][:, :][:, ::-1], m["rf"][:, :][:, ::-1], oh[:, :][:, ::-1], 0.0, ALU.mult, ALU.add))
    Z = m["Z"]
    ch(V.tensor_tensor(Z[:, :], m["zf"][:, :], m["zb"][:, :], ALU.add))
    ch(V.tensor_tensor(Z[:, :], Z[:, :], oh[:, :], ALU.subtract))
    ch(V.tensor_scalar(Z[:, :], Z[:, :], 1e15, -1e15, ALU.min, ALU.max))
    V.scalar_tensor_tensor(out=m["sq"][:, :], in0=Z[:, :], scalar=1.0, in1=Z[:, :], op0=ALU.mult, op1=ALU.mult,
                           accum_out=m["zc"][:, 2:3]).then_inc(S("znorm2"), 1)
    dve.wait_ge(S("znorm"), 1)
    ch(V.reciprocal(m["zc"][:, 4:5], m["zc"][:, 3:4]))
    V.tensor_scalar(Z[:, :], Z[:, :], m["zc"][:, 4:5], None, ALU.mult).then_inc(S("z_ready"), 1)
    dve.wait_ge(S("z_turned"), 1)
    V.tensor_copy(m["ZT"][:, :], ps[4][0:N, 0:N]).then_inc(S("zt_ready"), 1)
    dve.wait_ge(S("u_first"), 1)
    V.tensor_copy(m["Q"][:, :], ps[6][0:N, 0:N]).then_inc(own.sem, 1); own.n += 1
    V.tensor_copy(m["XT"][:, :], ps[6][0:N, N:2 * N]).then_inc(own.sem, 1); own.n += 1
    V.tensor_copy(m["X"][:, :], ps[5][0:N, 0:N]).then_inc(S("x_ready"), 1)

    R, zc = m["R"], m["zc"]
    for r in range(REFINE):
        dve.wait_ge(S("gram_ready"), r + 1)
        V.tensor_copy(m["AX"][:, :], ps[1][0:N, 0:N]).then_inc(S("ax_ready"), 1)
        ch(V.tensor_tensor(R[:, :], ident, ps[0][0:N, 0:N], ALU.subtract))
        ch(V.tensor_tensor(m["sq"][:, :], ident, ps[0][0:N, 0:N], ALU.mult))
        ch(V.tensor_reduce(zc[:, 5:6], m["sq"][:, :], AX.X, ALU.add))
        ch(V.reciprocal(zc[:, 5:6], zc[:, 5:6]))
        dve.wait_ge(S("s_ready"), r + 1)
        ch(V.tensor_tensor(m["sq"][:, :], ident, ps[2][0:N, 0:N], ALU.mult))
        ch(V.tensor_reduce(zc[:, 6:7], m["sq"][:, :], AX.X, ALU.add))
        ch(V.tensor_tensor(zc[:, 7:8], zc[:, 6:7], zc[:, 5:6], ALU.mult))
        V.tensor_scalar(m["LD"][:, :], ident, zc[:, 7:8], None, ALU.mult).then_inc(S("lamdiag_ready"), 1)
        dve.wait_ge(S("lamrow_ready"), r + 1)
        ch(V.tensor_scalar(m["den"][:, :], ps[3][0:N, 0:N], zc[:, 7:8], None, ALU.subtract))
        ch(V.tensor_tensor(m["num"][:, :], R[:, :], ps[3][0:N, 0:N], ALU.mult))
        ch(V.tensor_tensor(m["num"][:, :], m["num"][:, :], ps[2][0:N, 0:N], ALU.add))
        ch(V.tensor_scalar(m["mask"][:, :], m["den"][:, :], 0.0, 1.0 / BIG, ALU.is_equal, ALU.mult))
        ch(V.tensor_tensor(m["den"][:, :], m["den"][:, :], m["mask"][:, :], ALU.add))
        ch(V.reciprocal(m["den"][:, :], m["den"][:, :]))
        ch(V.tensor_scalar(m["den"][:, :], m["den"][:, :], BIG, -BIG, ALU.min, ALU.max))
        ch(V.tensor_tensor(m["E0"][:, :], m["num"][:, :], m["den"][:, :], ALU.mult))
        ch(V.tensor_tensor(m["mask"][:, :], m["E0"][:, :], m["E0"][:, :], ALU.mult))
        ch(V.tensor_scalar(m["mask"][:, :], m["mask"][:, :], 0.25, None, ALU.is_le))
        ch(V.tensor_tensor(m["E0"][:, :], m["E0"][:, :], m["mask"][:, :], ALU.mult))
        ch(V.tensor_scalar(R[:, :], R[:, :], 0.5, None, ALU.mult))
        ch(V.tensor_scalar(m["mask"][:, :], m["mask"][:, :], -1.0, 1.0, ALU.mult, ALU.add))
        ch(V.tensor_tensor(R[:, :], R[:, :], m["mask"][:, :], ALU.mult))
        ch(V.tensor_tensor(R[:, :], R[:, :], m["E0"][:, :], ALU.add))
        V.tensor_tensor(m["LD"][:, :], R[:, :], ident, ALU.add).then_inc(S("e_ready"), 1)
        dve.wait_ge(S("x_next"), r + 1)
        V.tensor_copy(m["XT"][:, :], ps[4][0:N, N:2 * N]).then_inc(own.sem, 1); own.n += 1
        V.tensor_copy(m["X"][:, :], ps[4][0:N, 0:N]).then_inc(S("x_ready"), 1)

    W, sc, sg = m["W"], m["sc"], m["sg"]
    dve.wait_ge(S("w_ready"), 1)
    ch(V.tensor_copy(W[:, :], ps[0][0:N, 0:N]))
    for a, cut in enumerate((31, 15, 47)):
        ch(V.tensor_scalar(sg[:, a:a + 1], EB[0:N, cut:cut + 1], 0.0, 2.0, ALU.is_ge, ALU.mult))
        ch(V.tensor_scalar(sg[:, a:a + 1], sg[:, a:a + 1], -1.0, None, ALU.add))
        ch(V.scalar_tensor_tensor(out=sc[:, a:a + 1], in0=W[:, cut + 1:cut + 2], scalar=sg[:, a:a + 1],
                                  in1=W[:, cut:cut + 1], op0=ALU.mult, op1=ALU.add))
    ch(V.tensor_tensor(sc[:, 3:4], sc[:, 0:1], EB[0:N, 31:32], ALU.mult))
    ch(V.tensor_tensor(sc[:, 3:4], sc[:, 3:4], sc[:, 3:4], ALU.mult))
    ch(V.tensor_tensor(sc[:, 4:5], m["lim"][0:N, 0:1], m["lim"][0:N, 1:2], ALU.max))
    ch(V.tensor_scalar(sc[:, 4:5], sc[:, 4:5], 7e-7 / 2 ** 0.5, None, ALU.mult))
    ch(V.tensor_tensor(sc[:, 4:5], sc[:, 4:5], sc[:, 4:5], ALU.mult))
    ch(V.tensor_tensor(sc[:, 5:6], sc[:, 3:4], sc[:, 4:5], ALU.is_gt))
    ch(V.scalar_tensor_tensor(out=m["sq"][:, 0:N // 2], in0=W[:, 0:N // 2], scalar=1.0, in1=W[:, 0:N // 2],
                              op0=ALU.mult, op1=ALU.mult, accum_out=sc[:, 6:7]))
    ch(V.tensor_scalar(sc[:, 7:8], sc[:, 6:7], 0.5, None, ALU.is_gt))
    for into, mask, yes, no in ((8, 7, 1, 2), (12, 5, 0, 8)):
        ch(V.tensor_scalar(sc[:, into + 1:into + 2], sc[:, mask:mask + 1], -1.0, 1.0, ALU.mult, ALU.add))
        ch(V.tensor_tensor(sc[:, into + 2:into + 3], sc[:, mask:mask + 1], sc[:, yes:yes + 1], ALU.mult))
        ch(V.tensor_tensor(sc[:, into + 1:into + 2], sc[:, into + 1:into + 2], sc[:, no:no + 1], ALU.mult))
        ch(V.tensor_tensor(sc[:, into:into + 1], sc[:, into + 1:into + 2], sc[:, into + 2:into + 3], ALU.add))
    ch(V.tensor_scalar(sc[:, 16:17], sc[:, 12:13], 0.0, 2.0, ALU.is_lt, ALU.mult))
    ch(V.tensor_scalar(sc[:, 17:18], sc[:, 16:17], -1.0, None, ALU.add))
    ch(V.tensor_scalar(m["UT2"][:, 0:N], m["XT"][:, :], sc[:, 17:18], None, ALU.mult))
    V.tensor_scalar(m["UT2"][:, N:P], m["XT"][:, :], sc[:, 17:18], None, ALU.mult).then_inc(S("ut_ready"), 1)
    dve.wait_ge(S("blocks_ready"), 1)
    for h in (0, N):
        ch(V.tensor_copy(UB[h:h + N, h:h + N], ps[1][h:h + N, 0:N]))
        ch(V.tensor_copy(UTB[h:h + N, h:h + N], ps[1][h:h + N, N:2 * N]))


def eig_tensor(nc, pe, S, C, m, ps):
    T = nc.tensor
    ident, ones = C[0:N, C_ID:C_ID + N], C[0:N, C_ONE:C_ONE + P]

    def mm(out, lhsT, rhs):
        return T.matmul(out, lhsT, rhs, start=True, stop=True)
    pe.wait_ge(S("const_in"), 16)
    pe.wait_ge(S("dinv_diag"), 1)
    pe.wait_ge(S("eig_dve"), 1)
    mm(ps[0][:, 0:P], ones, m["AI"][:, :])
    mm(ps[0][:, P:P + 1], C[0:N, C_DUP:C_DUP + P], m["c"][:, 5:6]).then_inc(S("dinv_rows"), 1)
    pe.wait_ge(S("lap_ready"), 1)
    T.transpose(ps[1][0:N, 0:N], m["H"][:, :], ident).then_inc(S("lap_turned"), 1)
    pe.wait_ge(S("lap_sym"), 1)
    T.transpose(ps[0][0:N, 0:N], m["L"][:, :], ident).then_inc(S("hh_pe"), 1)
    hd, hp, ha = S("hh_dve"), S("hh_pe"), S("hh_act")
    ND, NP, NA = 17, 6, 2
    with pe.Fori(0, STEPS) as k:
        b = k * ND
        hold(pe, hd, b + 3)
        mm(ps[1][0:N, 0:3], m["X3"][:, 0:1].to_broadcast([N, N]), m["X3"][:, 0:3]).then_inc(hp, 1)
        hold(pe, hd, b + 8)
        mm(ps[2][0:1, 0:N], m["v"][:, :], ident).then_inc(hp, 1)
        hold(pe, hd, b + 14)
        mm(ps[3][0:N, 0:N], m["rowv"][:, :], m["rowu"][:, :]).then_inc(hp, 1)
        hold(pe, hd, b + 15)
        hold(pe, ha, k * NA + 2)
        mm(ps[4][0:N, 0:N], m["tri"][:, :], m["H"][:, :]).then_inc(hp, 1)
        hold(pe, hd, b + 16)
        mm(ps[0][0:N, 0:N], m["H"][:, :], m["B"][:, :]).then_inc(hp, 1)
        mm(ps[5][0:N, 0:N], m["H"][:, :], m["QT"][:, :]).then_inc(hp, 1)
    pe.wait_ge(S("tri_parts"), 1)
    mm(ps[1][:, 0:P], ones, m["AI"][:, :]).then_inc(S("tri_rows"), 1)
    pe.wait_ge(S("lam_ready"), 1)
    mm(ps[2][:, 0:1], C[0:N, C_DUP:C_DUP + P], m["lim"][0:N, 6:7]).then_inc(S("lam_both"), 1)
    pe.wait_ge(S("pivots_ready"), 1)
    mm(ps[3][0:N, 0:N], C[:, C_ID + N:C_ID + P], m["PVC"][:, :]).then_inc(S("pivots_moved"), 1)
    pe.wait_ge(S("z_ready"), 1)
    T.transpose(ps[4][0:N, 0:N], m["Z"][:, :], ident).then_inc(S("z_turned"), 1)
    T.transpose(ps[6][0:N, 0:N], m["QT"][:, :], ident)
    pe.wait_ge(S("zt_ready"), 1)
    mm(ps[6][0:N, N:2 * N], m["ZT"][:, :], m["QT"][:, :])
    mm(ps[5][0:N, 0:N], m["QT"][:, :], m["ZT"][:, :]).then_inc(S("u_first"), 1)
    for r in range(REFINE):
        pe.wait_ge(S("x_ready"), r + 1)
        mm(ps[1][0:N, 0:N], m["L"][:, :], m["X"][:, :])
        mm(ps[0][0:N, 0:N], m["X"][:, :], m["X"][:, :]).then_inc(S("gram_ready"), 1)
        pe.wait_ge(S("ax_ready"), r + 1)
        mm(ps[2][0:N, 0:N], m["X"][:, :], m["AX"][:, :]).then_inc(S("s_ready"), 1)
        pe.wait_ge(S("lamdiag_ready"), r + 1)
        mm(ps[3][0:N, 0:N], ones[:, 0:N], m["LD"][:, :]).then_inc(S("lamrow_ready"), 1)
        pe.wait_ge(S("e_ready"), r + 1)
        mm(ps[4][0:N, N:2 * N], m["LD"][:, :], m["XT"][:, :])
        mm(ps[4][0:N, 0:N], m["XT"][:, :], m["LD"][:, :]).then_inc(S("x_next"), 1)
    pe.wait_ge(S("x_ready"), REFINE + 1)
    mm(ps[0][0:N, 0:N], m["X"][:, :], m["Q"][:, :]).then_inc(S("w_ready"), 1)
    pe.wait_ge(S("ut_ready"), 1)
    mm(ps[1][:, 0:N], m["UT2"][:, :], ident)
    mm(ps[1][:, N:2 * N], C[0:N, C_DUP:C_DUP + P], m["UT2"][:, 0:N]).then_inc(S("blocks_ready"), 1)


def eig_scalar(nc, act, S, m, ps):
    act.wait_ge(S("deg_ready"), 1)
    act.wait_ge(S("eig_dve"), 1)
    nc.scalar.activation(m["c"][:, 2:4], m["c"][:, 0:2], ACT.Sqrt).then_inc(S("deg_root"), 1)
    hd, ha = S("hh_dve"), S("hh_act")
    act.wait_ge(S("hh_pe"), 1)
    act.wait_ge(S("dinv_rows"), 1)
    with act.Fori(0, STEPS) as k:
        hold(act, hd, k * 17 + 4)
        nc.scalar.activation(m["c"][:, 7:8], m["S2"][:, 0:1], ACT.Sqrt).then_inc(ha, 1)
        nc.scalar.copy(m["tri"][:, :], ps[0][0:N, 0:N]).then_inc(ha, 1)
    act.wait_ge(S("znorm2"), 1)
    nc.scalar.activation(m["zc"][:, 3:4], m["zc"][:, 2:3], ACT.Sqrt).then_inc(S("znorm"), 1)



TILES = 16
PAIRS = 4
TOK = PAIRS * P
E8 = 8
HID0 = 341
CH0 = [(0, 128), (128, 128), (256, 85)]
CH1 = 4
EPS = 1e-5


def stage_gnn0(nc, eng, who, S, C, t, ps):
    X, XT = t["X"], t["xT"]
    ident = C[:, C_ID:C_ID + P]
    dv, pe_s, ac = S("g0_dve"), S("g0_pe"), S("g0_act")
    ND, NP, NA = 24, 4, 4
    with eng.Fori(0, TILES) as i:
        xt = X[:, bass.ds(i * PAIRS, PAIRS), :]

        def after(sem, per, n):
            hold(eng, sem, i * per + n)
        if who == "dve":
            V = nc.vector

            def layernorm(n):
                for q in range(PAIRS):
                    V.bn_stats(t["bn"][:, q, :], t["xw"][:, q, :]).then_inc(dv, 1)
                after(dv, ND, n + 4)
                for q in range(PAIRS):
                    V.bn_aggr(t["mv"][:, q, :], t["bn"][:, q, :]).then_inc(dv, 1)
                after(dv, ND, n + 8)
                V.tensor_scalar(t["sd"][:, 0:PAIRS], t["mv"][:, :, 1], EPS, None, ALU.add).then_inc(dv, 1)
            V.tensor_copy(t["xw"][:, :, :], xt).then_inc(dv, 1)
            after(dv, ND, 1)
            layernorm(1)
            after(ac, NA, 1)
            V.reciprocal(t["sd"][:, 8:8 + PAIRS], t["sd"][:, 4:4 + PAIRS]).then_inc(dv, 1)
            after(dv, ND, 11)
            for q in range(PAIRS):
                ins = V.tensor_scalar(t["xh"][:, q, :], t["xw"][:, q, :], t["mv"][:, q, 0:1], t["sd"][:, 8 + q:9 + q],
                                      ALU.subtract, ALU.mult)
            ins.then_inc(dv, 1)
            after(pe_s, NP, 3)
            V.tensor_tensor(t["gm"][:, :], ps[2][:, :], t["b2row"][:, :], ALU.add).then_inc(dv, 1)
            after(pe_s, NP, 4)
            V.tensor_tensor(t["xw"][:, :, :], t["xw"][:, :, :], ps[3][:, :].rearrange("p (q d) -> p q d", q=PAIRS),
                            ALU.add).then_inc(dv, 1)
            after(dv, ND, 14)
            V.tensor_copy(xt, t["xw"][:, :, :])
            layernorm(14)
            after(ac, NA, 4)
            V.reciprocal(t["sd"][:, 8:8 + PAIRS], t["sd"][:, 4:4 + PAIRS]).then_inc(dv, 1)
            after(dv, ND, 24)
            for q in range(PAIRS):
                ins = V.tensor_scalar(t["xh"][:, q, :], t["xw"][:, q, :], t["mv"][:, q, 0:1], t["sd"][:, 8 + q:9 + q],
                                      ALU.subtract, ALU.mult)
            ins.then_inc(S("g0_xh2"), 1)
            after(S("g0_turned"), 1, 1)
            V.tensor_copy(XT[:, bass.ds(i * TOK, TOK)], ps[4][:, :]).then_inc(S("g0_xt"), 1)
        if who == "pe":
            T = nc.tensor
            after(dv, ND, 12)
            for q in range(PAIRS):
                ins = T.matmul(ps[0][:, q * P:(q + 1) * P], t["xh"][:, q, :], t["UB"][:, :], start=True, stop=True)
            ins.then_inc(pe_s, 1)
            after(ac, NA, 2)
            T.matmul(ps[1][:, :], t["w1g0"][:, :], t["ga"][:, :], start=True, stop=True).then_inc(pe_s, 1)
            after(ac, NA, 3)
            for q in range(PAIRS):
                ins = T.matmul(ps[2][:, q * P:(q + 1) * P], t["gh"][:, q * P:(q + 1) * P], t["w2g0"][:, :],
                               start=True, stop=True)
            ins.then_inc(pe_s, 1)
            after(dv, ND, 13)
            T.matmul(ps[3][:, :], t["UTB"][:, :], t["gm"][:, :], start=True, stop=True).then_inc(pe_s, 1)
            after(S("g0_xh2"), 1, 1)
            for q in range(PAIRS):
                ins = T.transpose(ps[4][:, q * P:(q + 1) * P], t["xh"][:, q, :], ident)
            ins.then_inc(S("g0_turned"), 1)
        if who == "act":
            A = nc.scalar
            after(dv, ND, 10)
            A.activation(t["sd"][:, 4:4 + PAIRS], t["sd"][:, 0:PAIRS], ACT.Sqrt).then_inc(ac, 1)
            after(pe_s, NP, 1)
            A.copy(t["ga"][:, :], ps[0][:, :]).then_inc(ac, 1)
            after(pe_s, NP, 2)
            A.activation(t["gh"][:, :], ps[1][:, :], ACT.Relu, bias=t["b1g0"][:, 0:1]).then_inc(ac, 1)
            after(dv, ND, 23)
            A.activation(t["sd"][:, 4:4 + PAIRS], t["sd"][:, 0:PAIRS], ACT.Sqrt).then_inc(ac, 1)


def stage_route(nc, eng, who, S, C, t, ps, layer):
    XT = t["xT"]
    ident = C[:, C_ID:C_ID + P]
    s = lambda n: S(f"r{layer}_{n}")
    dv = s("dve")
    ND = 25
    W = PAIRS * E8
    a, b, o1, o2, sc = (t["rt"][:, k, :] for k in range(5))
    v = lambda x: x.rearrange("p (q e) -> p q e", q=PAIRS)
    cols = lambda k: t["rc"][:, k, :]
    if who == "pe":
        eng.sem_inc(s("turned"), 1)
    if who == "sp":
        eng.sem_inc(s("gates_out"), 1)
    wide = lambda k: cols(k).unsqueeze(2).to_broadcast([P, PAIRS, E8])
    with eng.Fori(0, TILES) as i:
        def after(sem, per, n):
            hold(eng, sem, i * per + n)
        if who == "dve":
            V = nc.vector
            at = [0]

            def go(ins):
                at[0] += 1
                ins.then_inc(dv, 1)
                after(dv, ND, at[0])
            after(s("turned"), 1, 1)
            go(V.tensor_copy(t["xr"][:, :], XT[:, bass.ds(i * TOK, TOK)]))
            after(s("logits"), 1, 1)
            go(V.tensor_copy(a, ps[0][:, 0:W]))
            go(V.tensor_reduce(cols(0), v(a), AX.X, ALU.max))
            go(V.tensor_tensor(v(a), v(a), wide(0), ALU.subtract))
            after(s("exp"), 1, 1)
            go(V.tensor_reduce(cols(1), v(b), AX.X, ALU.add))
            go(V.reciprocal(cols(2), cols(1)))
            go(V.tensor_tensor(v(b), v(b), wide(2), ALU.mult))
            cols_of = C[:, C_EXP:C_EXP + W]
            for o, src in ((o1, b), (o2, a)):
                go(V.tensor_reduce(cols(3), v(src), AX.X, ALU.max))
                go(V.tensor_tensor(v(o), v(src), wide(3), ALU.is_equal))
                go(V.tensor_tensor(sc, o, cols_of, ALU.mult))
                go(V.tensor_reduce(cols(4), v(sc), AX.X, ALU.max))
                go(V.tensor_tensor(v(o), v(sc), wide(4), ALU.is_equal))
                if o is o1:
                    go(V.scalar_tensor_tensor(out=a, in0=o1, scalar=-2.0, in1=b, op0=ALU.mult, op1=ALU.add))
            go(V.tensor_tensor(o1, o1, o2, ALU.add))
            go(V.tensor_tensor(b, b, o1, ALU.mult))
            go(V.tensor_reduce(cols(5), v(b), AX.X, ALU.add))
            if layer == 0:
                go(V.tensor_scalar(cols(5), cols(5), 1e-9, None, ALU.add))
            else:
                go(V.tensor_copy(cols(5), cols(5)))
            go(V.reciprocal(cols(6), cols(5)))
            go(V.tensor_tensor(v(b), v(b), wide(6), ALU.mult))
            assert at[0] == ND - 1, at
            after(s("turned"), 1, 2)
            after(s("gates_out"), 16, 1)
            V.tensor_copy(t["gT"][:, :], ps[1][0:E8, :]).then_inc(dv, 1)
        if who == "pe":
            T = nc.tensor
            after(dv, ND, 1)
            for q in range(PAIRS):
                ins = T.matmul(ps[0][:, q * E8:(q + 1) * E8], t["xr"][:, q * P:(q + 1) * P], t[f"wr{layer}"][:, :],
                               start=True, stop=True)
            ins.then_inc(s("logits"), 1)
            after(dv, ND, ND - 1)
            for q in range(PAIRS):
                ins = T.transpose(ps[1][0:E8, q * P:(q + 1) * P], b[:, q * E8:(q + 1) * E8], ident)
            ins.then_inc(s("turned"), 1)
        if who == "act":
            after(dv, ND, 4)
            nc.scalar.activation(b, a, ACT.Exp).then_inc(s("exp"), 1)
        if who == "sp":
            after(dv, ND, ND)
            eng.dma_start(t[f"gates{layer}"][:, bass.ds(i * TOK, TOK)], t["gT"][:, :]).then_inc(s("gates_out"), 16)


def stage_experts(nc, eng, who, S, C, t, ps, layer, out=None):
    X, XT = t["X"], t["xT"]
    ident = C[:, C_ID:C_ID + P]
    s = lambda n: S(f"f{layer}_{n}")
    units = [(e, c) for e in range(E8) for c in range(3)] if layer == 0 else \
            [(e, c) for e in range(E8 + 1) for c in range(CH1)]
    NU = len(units)
    GB = t["GB"]
    NB = 2 if layer == 0 else 3
    HALF = TILES // 2

    SEEDED = NU + 1
    if who == "dve":
        for n in ("gated", "y_added"):
            eng.sem_inc(s(n), SEEDED)
    if who == "act":
        eng.sem_inc(s("act"), SEEDED)
    if who == "pe":
        eng.sem_inc(s("down"), SEEDED)
        eng.sem_inc(s("y_sum"), SEEDED)
    if who == "pool":
        eng.sem_inc(s("xo_free"), SEEDED)
    SEED = {s(n).name: SEEDED for n in ("gated", "y_added", "act", "down", "y_sum", "xo_free")}

    def wide_of(u):
        return CH0[units[u][1]][1] if layer == 0 else P
    with eng.Fori(0, HALF) as it:
        for par in range(2):
            tile = it * 2 + par
            tk = bass.ds(it * (2 * TOK) + par * TOK, TOK)

            def after(sem, per, n, par=par):
                hold(eng, sem, it * (2 * per) + (par * per + n + SEED.get(sem.name, 0)))
            if who == "sp":
                after(s("gated"), NU, -NU)
                for e in range(E8):
                    eng.dma_start(GB[:, par, e, :], t[f"gates{layer}"][e:e + 1, tk].to_broadcast([P, TOK])
                                  ).then_inc(S(f"f{layer}_gates{par}"), 16)
                if layer == 1:
                    after(s("y_sum"), 1, -1)
                    eng.dma_start(t["g9"][:, par, :], t["gates1"][:, tk]).then_inc(S(f"f1_gates{par}"), 16)
            NG = E8 + layer
            if who == "pe":
                T = nc.tensor
                y = ps[4 + par]

                def up(u):
                    e, c = units[u]
                    w = wide_of(u)
                    if layer == 0:
                        after(s("gated"), NU, u - 1)
                        T.matmul(ps[u % 2][0:w, :], t["w1f0"][:, e, CH0[c][0]:CH0[c][0] + w], XT[:, tk],
                                 start=True, stop=True)
                        T.matmul(ps[2 + u % 2][0:w, :], t["w3f0"][:, e, CH0[c][0]:CH0[c][0] + w], XT[:, tk],
                                 start=True, stop=True).then_inc(s("up"), 1)
                    else:
                        after(s("act"), NU, u - 3)
                        T.matmul(ps[u % 4][:, :], t["w1f1"][:, e, c * P:(c + 1) * P], XT[:, tk],
                                 start=True, stop=True).then_inc(s("up"), 1)

                def down(u):
                    e, c = units[u]
                    w = wide_of(u)
                    after(s("gated"), NU, u + 1)
                    src = t["hg"][:, u % 4, :]
                    wt = t[f"w2f{layer}"]
                    last = layer == 0 and u == NU - 1
                    ins = T.matmul(y[:, :], wt[0:w, e, c, :], src[0:w, :], start=(u == 0), stop=last,
                                   skip_group_check=True)
                    ins.then_inc(s("down"), 1)
                    return ins
                for u in range(NU + 1):
                    if u < NU:
                        up(u)
                    if u >= 1:
                        down(u - 1)
                if layer == 1:
                    hold(eng, S(f"f1_gates{par}"), it * (16 * NG) + 16 * NG)
                    T.matmul(y[:, :], t["b2p"][:, :], t["g9"][:, par, :], start=False, stop=True,
                             skip_group_check=True).then_inc(s("y_sum"), 1)
                else:
                    T.nop().then_inc(s("y_sum"), 1)
                after(s("y_copied"), 1, 1)
                after(s("y_added"), 1, -1)
                for q in range(PAIRS):
                    ins = T.transpose(ps[6 + par][:, q * P:(q + 1) * P], t["ysb"][:, q * P:(q + 1) * P], ident)
                ins.then_inc(s("y_turned"), 1)
            if who == "act":
                A = nc.scalar
                for u in range(NU):
                    e, c = units[u]
                    w = wide_of(u)
                    after(s("up"), NU, u + 1)
                    if layer == 0:
                        A.activation(t["hs"][0:w, u % 2, :], ps[u % 2][0:w, :], ACT.Silu).then_inc(s("act"), 1)
                    else:
                        dst = t["hs"][:, u % 2, :]
                        after(s("gated"), NU, u - 1)
                        A.activation(dst, ps[u % 4][:, :], ACT.Gelu,
                                     bias=t["b1f1"][:, e * CH1 + c:e * CH1 + c + 1]).then_inc(s("act"), 1)
            if who == "dve":
                V = nc.vector
                for u in range(NU):
                    e, c = units[u]
                    w = wide_of(u)
                    after(s("act"), NU, u + 1)
                    after(s("down"), NU, u - 3)
                    dst = t["hg"][0:w, u % 4, :]
                    if c == 0 and e < E8:
                        hold(eng, S(f"f{layer}_gates{par}"), it * (16 * NG) + 16 * NG) if e == 0 else None
                    if layer == 0:
                        V.tensor_tensor(t["ht"][u % 2][0:w, :], t["hs"][0:w, u % 2, :], ps[2 + u % 2][0:w, :],
                                        ALU.mult).then_inc(s("ht"), 1)
                        after(s("ht"), NU, u + 1)
                        V.tensor_tensor(dst, t["ht"][u % 2][0:w, :], GB[0:w, par, e, :], ALU.mult).then_inc(s("gated"), 1)
                    elif e < E8:
                        V.tensor_tensor(dst, t["hs"][:, u % 2, :], GB[:, par, e, :], ALU.mult).then_inc(s("gated"), 1)
                    else:
                        V.tensor_copy(dst, t["hs"][:, u % 2, :]).then_inc(s("gated"), 1)
                after(s("y_sum"), 1, 1)
                after(s("down"), NU, NU)
                if layer == 0:
                    V.tensor_copy(t["ysb"][:, :], ps[4 + par][:, :]).then_inc(s("y_copied"), 1)
                else:
                    V.tensor_scalar(t["ysb"][:, :], ps[4 + par][:, :], t["b2s"][:, 0:1], None,
                                    ALU.add).then_inc(s("y_copied"), 1)
                after(s("y_turned"), 1, 1)
                xt = X[:, bass.ds(it * (2 * PAIRS) + par * PAIRS, PAIRS), :]
                if layer == 1:
                    after(s("xo_free"), 1, -1)
                xo = t["xo"][:, par, :, :]
                V.tensor_tensor(xo, ps[6 + par][:, :].rearrange("p (q d) -> p q d", q=PAIRS), xt,
                                ALU.add).then_inc(s("y_added"), 1)
                if layer == 0:
                    after(s("y_added"), 1, 1)
                    V.tensor_copy(xt, xo).then_inc(s("x_kept"), 1)
                    after(s("x_kept"), 1, 1)
            if who == "pool" and layer == 1:
                after(s("y_added"), 1, 1)
                eng.dma_start(out[:, bass.ds(it * (2 * PAIRS) + par * PAIRS, PAIRS), :],
                              t["xo"][:, par, :, :]).then_inc(s("stored"), 16)
                after(s("stored"), 16, 16)
                eng.sem_inc(s("xo_free"), 1)


def stage_gnn1_mix(nc, eng, who, S, C, t, ps):
    X = t["X"]
    dv, pe_s, ac = S("a1_dve"), S("a1_pe"), S("a1_act")
    ND, NP, NA = 13, 3, 4
    with eng.Fori(0, TILES) as i:
        tk = bass.ds(i * TOK, TOK)

        def after(sem, per, n):
            hold(eng, sem, i * per + n)
        if who == "dve":
            V = nc.vector
            V.tensor_copy(t["xw"][:, :, :], X[:, bass.ds(i * PAIRS, PAIRS), :]).then_inc(dv, 1)
            after(dv, ND, 1)
            for q in range(PAIRS):
                V.bn_stats(t["bn"][:, q, :], t["xw"][:, q, :]).then_inc(dv, 1)
            after(dv, ND, 5)
            for q in range(PAIRS):
                V.bn_aggr(t["mv"][:, q, :], t["bn"][:, q, :]).then_inc(dv, 1)
            after(dv, ND, 9)
            V.tensor_scalar(t["sd"][:, 0:PAIRS], t["mv"][:, :, 1], EPS, None, ALU.add).then_inc(dv, 1)
            after(ac, NA, 1)
            V.reciprocal(t["sd"][:, 8:8 + PAIRS], t["sd"][:, 4:4 + PAIRS]).then_inc(dv, 1)
            after(dv, ND, 11)
            for q in range(PAIRS):
                ins = V.tensor_scalar(t["xh"][:, q, :], t["xw"][:, q, :], t["mv"][:, q, 0:1], t["sd"][:, 8 + q:9 + q],
                                      ALU.subtract, ALU.mult)
            ins.then_inc(dv, 1)
            after(ac, NA, 4)
            for c in range(2):
                ins = V.bn_stats(t["bnh"][:, c, bass.ds(i * 6, 6)], t["HP"][:, c, tk])
            ins.then_inc(dv, 1)
        if who == "pe":
            T = nc.tensor
            after(dv, ND, 12)
            for q in range(PAIRS):
                ins = T.matmul(ps[0][:, q * P:(q + 1) * P], t["xh"][:, q, :], t["AHB"][:, :], start=True, stop=True)
            ins.then_inc(pe_s, 1)
            after(ac, NA, 2)
            for c in range(2):
                T.matmul(ps[1 + c][:, :], t["w1g1"][:, c * P:(c + 1) * P], t["ga"][:, :], start=True,
                         stop=True).then_inc(pe_s, 1)
        if who == "act":
            A = nc.scalar
            after(dv, ND, 10)
            A.activation(t["sd"][:, 4:4 + PAIRS], t["sd"][:, 0:PAIRS], ACT.Sqrt).then_inc(ac, 1)
            after(pe_s, NP, 1)
            A.copy(t["ga"][:, :], ps[0][:, :]).then_inc(ac, 1)
            for c in range(2):
                after(pe_s, NP, 2 + c)
                A.activation(t["HP"][:, c, tk], ps[1 + c][:, :], ACT.Identity,
                             bias=t["b1g1"][:, c:c + 1]).then_inc(ac, 1)


def batch_norm(nc, eng, who, S, t, n, chunks, stats, gamma, beta, out):
    if who == "dve":
        V = nc.vector
        own = Count(eng, S(f"bn{n}_dve"))
        eng.wait_ge(S(f"bn{n}_stats"), 1)
        for c in range(chunks):
            own.chain(V.bn_aggr(t["bmv"][:, c, :], stats[:, c, :]))
        V.tensor_scalar(t["bsd"][:, 0:chunks], t["bmv"][:, 0:chunks, 1], EPS, None, ALU.add).then_inc(S(f"bn{n}_var"), 1)
        eng.wait_ge(S(f"bn{n}_root"), 1)
        own.chain(V.reciprocal(t["bsd"][:, 4:4 + chunks], t["bsd"][:, 2:2 + chunks]))
        own.chain(V.tensor_tensor(out[:, 0, :], t["bsd"][:, 4:4 + chunks], gamma, ALU.mult))
        own.chain(V.tensor_tensor(t["bsd"][:, 6:6 + chunks], t["bmv"][:, 0:chunks, 0], out[:, 0, :], ALU.mult))
        V.tensor_tensor(out[:, 1, :], beta, t["bsd"][:, 6:6 + chunks], ALU.subtract).then_inc(S(f"bn{n}_ready"), 1)
    if who == "act":
        eng.wait_ge(S(f"bn{n}_var"), 1)
        nc.scalar.activation(t["bsd"][:, 2:2 + chunks], t["bsd"][:, 0:chunks], ACT.Sqrt).then_inc(S(f"bn{n}_root"), 1)


def stage_gnn1_out(nc, eng, who, S, C, t, ps):
    dv, pe_s, ac = S("b1_dve"), S("b1_pe"), S("b1_act")
    with eng.Fori(0, TILES) as i:
        tk = bass.ds(i * TOK, TOK)

        def after(sem, per, n):
            hold(eng, sem, i * per + n)
        if who == "dve":
            after(ac, 3, 3)
            nc.vector.bn_stats(t["bno"][:, 0, bass.ds(i * 6, 6)], t["xT"][:, tk]).then_inc(dv, 1)
        if who == "pe":
            after(ac, 3, 2)
            nc.tensor.matmul(ps[0][:, :], t["w2g1"][:, 0, :], t["gh"][:, :], start=True, stop=False)
            nc.tensor.matmul(ps[0][:, :], t["w2g1"][:, 1, :], t["ga"][:, :], start=False, stop=True).then_inc(pe_s, 1)
        if who == "act":
            for c, dst in enumerate((t["gh"], t["ga"])):
                nc.scalar.activation(dst[:, :], t["HP"][:, c, tk], ACT.Relu, bias=t["bn1"][:, 1, c:c + 1],
                                     scale=t["bn1"][:, 0, c:c + 1]).then_inc(ac, 1)
            after(pe_s, 1, 1)
            nc.scalar.activation(t["xT"][:, tk], ps[0][:, :], ACT.Identity, bias=t["b2g1"][:, 0:1]).then_inc(ac, 1)


def stage_gnn1_add(nc, eng, who, S, C, t, ps):
    X, XT = t["X"], t["xT"]
    ident = C[:, C_ID:C_ID + P]
    dv, pe_s, ac = S("c1_dve"), S("c1_pe"), S("c1_act")
    ND, NP, NA = 15, 2, 1
    with eng.Fori(0, TILES) as i:
        tk = bass.ds(i * TOK, TOK)
        xt = X[:, bass.ds(i * PAIRS, PAIRS), :]

        def after(sem, per, n):
            hold(eng, sem, i * per + n)
        if who == "dve":
            V = nc.vector
            V.tensor_scalar(t["gm"][:, :], XT[:, tk], t["bn2"][:, 0, 0:1], t["bn2"][:, 1, 0:1], ALU.mult,
                            ALU.add).then_inc(dv, 1)
            after(pe_s, NP, 1)
            V.tensor_tensor(t["xw"][:, :, :], ps[0][:, :].rearrange("p (q d) -> p q d", q=PAIRS), xt,
                            ALU.add).then_inc(dv, 1)
            after(dv, ND, 2)
            V.tensor_copy(xt, t["xw"][:, :, :])
            for q in range(PAIRS):
                V.bn_stats(t["bn"][:, q, :], t["xw"][:, q, :]).then_inc(dv, 1)
            after(dv, ND, 6)
            for q in range(PAIRS):
                V.bn_aggr(t["mv"][:, q, :], t["bn"][:, q, :]).then_inc(dv, 1)
            after(dv, ND, 10)
            V.tensor_scalar(t["sd"][:, 0:PAIRS], t["mv"][:, :, 1], EPS, None, ALU.add).then_inc(dv, 1)
            after(ac, NA, 1)
            V.reciprocal(t["sd"][:, 8:8 + PAIRS], t["sd"][:, 4:4 + PAIRS]).then_inc(dv, 1)
            after(dv, ND, 12)
            for q in range(PAIRS):
                ins = V.tensor_scalar(t["xh"][:, q, :], t["xw"][:, q, :], t["mv"][:, q, 0:1], t["sd"][:, 8 + q:9 + q],
                                      ALU.subtract, ALU.mult)
            ins.then_inc(dv, 1)
            after(pe_s, NP, 2)
            V.tensor_copy(XT[:, tk], ps[1][:, :]).then_inc(dv, 1)
            after(dv, ND, 14)
            V.engine_nop().then_inc(dv, 1)
        if who == "pe":
            T = nc.tensor
            for n, (src, k) in enumerate((("gm", 1), ("xh", 13))):
                after(dv, ND, k)
                for q in range(PAIRS):
                    block = t[src][:, q * P:(q + 1) * P] if src == "gm" else t[src][:, q, :]
                    ins = T.transpose(ps[n][:, q * P:(q + 1) * P], block, ident)
                ins.then_inc(pe_s, 1)
        if who == "act":
            after(dv, ND, 11)
            nc.scalar.activation(t["sd"][:, 4:4 + PAIRS], t["sd"][:, 0:PAIRS], ACT.Sqrt).then_inc(ac, 1)


WREG = 2 * E8 * HID0 + E8 * 3 * P
WREG1 = (E8 + 1) * CH1 * P * 2
HPW = 2 * TILES * TOK


def build(nc, d, out, gates):
    with ExitStack() as ctx:
        def sb(name, shape):
            return ctx.enter_context(nc.sbuf_tensor(name, shape, F32))
        sems = {}

        def S(name):
            if name not in sems:
                sems[name] = ctx.enter_context(nc.semaphore(name))
            return sems[name]
        ps = [ctx.enter_context(nc.psum_tensor(f"bank{i}", [P, 512], F32)) for i in range(8)]
        C = sb("consts", [P, C_COLS])
        hp = sb("hp", [P, HPW])
        wreg = sb("wreg", [P, max(WREG, WREG1)])
        t = dict(gates0=gates[0], gates1=gates[1])
        for name, shape in dict(
            X=[P, N, D], xT=[P, TILES * TOK], UB=[P, P], UTB=[P, P], AHB=[P, P],
            w1g0=[P, P], w2g0=[P, P], b1g0=[P, 1], b2row=[P, TOK], wr0=[P, E8], wr1=[P, E8],
            w1g1=[P, 2 * P], b1g1=[P, 2], w2g1=[P, 2, P], b2g1=[P, 1], gb1=[P, 4], gb2=[P, 2],
            b1f1=[P, (E8 + 1) * CH1], b2p=[E8, P], b2s=[P, 1],
            xw=[P, PAIRS, D], xh=[P, PAIRS, D], gm=[P, TOK], ga=[P, TOK], gh=[P, TOK],
            bn=[P, PAIRS, 6], mv=[P, PAIRS, 2], sd=[P, 12], bnh=[P, 2, TILES * 6], bno=[P, 1, TILES * 6],
            bmv=[P, 2, 2], bsd=[P, 8], bn1=[P, 2, 2], bn2=[P, 2, 1],
            rt=[P, 5, PAIRS * E8], rc=[P, 7, PAIRS], gT=[E8, TOK],
        ).items():
            t[name] = sb(name, shape)
        t["xr"], t["ht"] = t["gm"], (t["gm"], t["gh"])
        t["ysb"] = t["ga"]
        t["HP"] = hp[:, :].rearrange("p (c t) -> p c t", c=2)
        t["GB"] = hp[:, 0:2 * E8 * TOK].rearrange("p (b e t) -> p b e t", b=2, e=E8)
        upper = 2 * E8 * TOK

        def part(rows, n, start):
            return hp[0:rows, upper + start * TOK:upper + (start + n) * TOK].rearrange("p (n t) -> p n t", n=n)
        t["g9"], t["hs"], t["hg"] = part(E8, 2, 0), part(P, 2, 2), part(P, 4, 4)
        t["xo"] = hp[:, upper + 8 * TOK:upper + 10 * TOK].rearrange("p (b q d) -> p b q d", b=2, q=PAIRS)
        at = [0]

        def piece(name, shape):
            w = shape[1]
            at[0] += w
            return hp[0:shape[0], at[0] - w:at[0]]
        m = eig_memory(piece, None)
        n1 = E8 * HID0
        t["w1f0"] = wreg[:, 0:n1].rearrange("p (e h) -> p e h", e=E8)
        t["w3f0"] = wreg[:, n1:2 * n1].rearrange("p (e h) -> p e h", e=E8)
        t["w2f0"] = wreg[:, 2 * n1:2 * n1 + E8 * 3 * P].rearrange("p (e c d) -> p e c d", e=E8, c=3)
        half = WREG1 // 2
        t["w1f1"] = wreg[:, 0:half].rearrange("p (e f) -> p e f", e=E8 + 1)
        t["w2f1"] = wreg[:, half:2 * half].rearrange("p (e c d) -> p e c d", e=E8 + 1, c=CH1)
        block = ctx.enter_context(nc.Block())

        def program(eng, who):
            if who == "dve":
                eig_vector(nc, eng, S, C, m, ps, 0, 0, t["UB"], t["UTB"], t["AHB"])
                eng.wait_ge(S("x_in"), 32)
                eng.wait_ge(S("small_in"), SMALL)
            if who == "pe":
                eig_tensor(nc, eng, S, C, m, ps)
                eng.wait_ge(S("small_in"), SMALL)
            if who == "act":
                eig_scalar(nc, eng, S, m, ps)
                eng.wait_ge(S("small_in"), SMALL)
            stage_gnn0(nc, eng, who, S, C, t, ps)
            stage_route(nc, eng, who, S, C, t, ps, 0)
            if who == "sp":
                eng.wait_ge(S("r0_gates_out"), 16 * TILES + 1)
            if who == "pe":
                eng.wait_ge(S("w0_in"), W0)
                eng.wait_ge(S("r0_dve"), 25 * TILES)
            stage_experts(nc, eng, who, S, C, t, ps, 0)
            if who == "sp":
                eng.wait_ge(S("f0_down"), E8 * 3 * (TILES + 1) + 1)
                half = (E8 + 1) * CH1 * P
                eng.dma_start(t["w1f1"][:, 0:E8, :], d["w1p"]).then_inc(S("w1_in"), 16)
                eng.dma_start(t["w1f1"][:, E8, :], d["w1s"]).then_inc(S("w1_in"), 16)
                for e in range(E8):
                    eng.dma_start(t["w2f1"][:, e, :, :], d["w2p"][e].rearrange("(c f) d -> f c d", f=P)
                                  ).then_inc(S("w1_in"), 16)
                eng.dma_start(t["w2f1"][:, E8, :, :], d["w2s"].rearrange("(c f) d -> f c d", f=P)
                              ).then_inc(S("w1_in"), 16)
            stage_gnn1_mix(nc, eng, who, S, C, t, ps)
            if who == "dve":
                eng.wait_ge(S("a1_dve"), 13 * TILES)
                eng.nop().then_inc(S("bn1_stats"), 1)
            batch_norm(nc, eng, who, S, t, 1, 2, t["bnh"], t["gb1"][:, 0:2], t["gb1"][:, 2:4], t["bn1"])
            if who == "act":
                eng.wait_ge(S("bn1_ready"), 1)
            stage_gnn1_out(nc, eng, who, S, C, t, ps)
            if who == "dve":
                eng.wait_ge(S("b1_dve"), TILES)
                eng.nop().then_inc(S("bn2_stats"), 1)
            batch_norm(nc, eng, who, S, t, 2, 1, t["bno"], t["gb2"][:, 0:1], t["gb2"][:, 1:2], t["bn2"])
            if who == "dve":
                eng.wait_ge(S("bn2_ready"), 1)
            stage_gnn1_add(nc, eng, who, S, C, t, ps)
            stage_route(nc, eng, who, S, C, t, ps, 1)
            if who == "sp":
                eng.wait_ge(S("r1_gates_out"), 16 * TILES + 1)
            if who == "pe":
                eng.wait_ge(S("w1_in"), 16 * (E8 + 3))
                eng.wait_ge(S("r1_dve"), 25 * TILES)
            stage_experts(nc, eng, who, S, C, t, ps, 1, out)
            if who == "pool":
                eng.wait_ge(S("f1_stored"), 16 * TILES)

        small = [
            (t["w1g0"][:, :], d["w1g0"]), (t["w2g0"][:, :], d["w2g0"]), (t["b1g0"][:, :], d["b1g0"]),
            *[(t["b2row"][:, q * P:(q + 1) * P], d["b2g0"].to_broadcast([P, P])) for q in range(PAIRS)],
            (t["wr0"][:, :], d["wr0"]), (t["wr1"][:, :], d["wr1"]), (t["w1g1"][:, :], d["w1g1"]),
            (t["b1g1"][:, :], d["b1g1"]), (t["w2g1"][:, :, :], d["w2g1"].rearrange("(c f) d -> f c d", f=P)),
            (t["b2g1"][:, :], d["b2g1"]),
            (t["gb1"][:, 0:2], d["g1"]), (t["gb1"][:, 2:4], d["be1"]), (t["gb2"][:, 0:1], d["g2"]),
            (t["gb2"][:, 1:2], d["be2"]), (t["b1f1"][:, 0:E8 * CH1], d["b1p"]),
            (t["b1f1"][:, E8 * CH1:], d["b1s"]), (t["b2p"][:, :], d["b2p"]), (t["b2s"][:, :], d["b2s"]),
        ]
        SMALL = 16 * len(small)
        W0 = 16 * 5

        @block.sync
        def _(sp):
            sp.dma_start(C[:, :], d["consts"]).then_inc(S("const_in"), 16)
            sp.dma_start(m["A"], d["adj"]).then_inc(S("adj_in"), 16)
            sp.dma_start(m["AT"][0:N, :], d["adjT"]).then_inc(S("adj_in"), 16)
            sp.dma_start(m["AT"][N:P, :], d["adjT"]).then_inc(S("adj_in"), 16)
            for h in range(2):
                sp.dma_start(t["X"][h * N:(h + 1) * N, :, :],
                             d["x"].rearrange("(p two) n d -> two n p d", two=2)[h]).then_inc(S("x_in"), 16)
            for dst, src in small:
                sp.dma_start(dst, src).then_inc(S("small_in"), 16)
            sp.dma_start(t["w1f0"], d["w1f0"]).then_inc(S("w0_in"), 16)
            sp.dma_start(t["w3f0"], d["w3f0"]).then_inc(S("w0_in"), 16)
            for c, (a, w) in enumerate(CH0):
                sp.dma_start(t["w2f0"][0:w, :, c, :], d["w2f0"][a:a + w]).then_inc(S("w0_in"), 16)
            program(sp, "sp")

        @block.tensor
        def _(pe):
            program(pe, "pe")

        @block.vector
        def _(dve):
            program(dve, "dve")

        @block.scalar
        def _(act):
            program(act, "act")

        @block.gpsimd
        def _(pool):
            program(pool, "pool")


def kernel(x, adj, L0_gnn_W1, L0_gnn_b1, L0_gnn_W2, L0_gnn_b2, L0_ffn_router_w, L0_ffn_w1, L0_ffn_w2, L0_ffn_w3,
           L1_gnn_W1, L1_gnn_b1, L1_gnn_g1, L1_gnn_be1, L1_gnn_W2, L1_gnn_b2, L1_gnn_g2, L1_gnn_be2,
           L1_ffn_Wr, L1_ffn_W1s, L1_ffn_b1s, L1_ffn_W2s, L1_ffn_b2s, L1_ffn_W1p, L1_ffn_b1p, L1_ffn_W2p, L1_ffn_b2p):
    import concourse.bacc as bacc
    from concourse.bass_utils import run_bass_kernel_spmd
    A = np.asarray

    def column(a, n=1):
        return A(a).reshape(n, P).T
    arrays = dict(
        consts=constants(), x=A(x), adj=A(adj), adjT=A(adj).T,
        w1g0=A(L0_gnn_W1), b1g0=column(L0_gnn_b1), w2g0=A(L0_gnn_W2), b2g0=A(L0_gnn_b2).reshape(1, P),
        wr0=A(L0_ffn_router_w).T, w1f0=A(L0_ffn_w1).transpose(2, 0, 1), w3f0=A(L0_ffn_w3).transpose(2, 0, 1),
        w2f0=A(L0_ffn_w2).transpose(2, 0, 1),
        w1g1=A(L1_gnn_W1).T, b1g1=column(L1_gnn_b1, 2), g1=column(L1_gnn_g1, 2), be1=column(L1_gnn_be1, 2),
        w2g1=A(L1_gnn_W2).T, b2g1=column(L1_gnn_b2), g2=column(L1_gnn_g2), be2=column(L1_gnn_be2),
        wr1=A(L1_ffn_Wr), w1s=A(L1_ffn_W1s), b1s=column(L1_ffn_b1s, CH1), w2s=A(L1_ffn_W2s), b2s=column(L1_ffn_b2s),
        w1p=A(L1_ffn_W1p).transpose(1, 0, 2), b1p=column(L1_ffn_b1p, E8 * CH1), w2p=A(L1_ffn_W2p), b2p=A(L1_ffn_b2p),
    )
    arrays = {f"in_{k}": np.ascontiguousarray(v) for k, v in arrays.items()}
    nc = bacc.Bacc("TRN2", target_bir_lowering=False, num_devices=1)
    d = {k[3:]: nc.dram_tensor(k, v.shape, F32, kind="ExternalInput").ap() for k, v in arrays.items()}
    out = nc.dram_tensor("out", (N, P, D), F32, kind="ExternalOutput").ap()
    gates = [nc.dram_tensor(f"gates{n}", (E8, TILES * TOK), F32).ap() for n in range(2)]
    build(nc, d, out.rearrange("q r d -> r q d"), gates)
    r = run_bass_kernel_spmd(nc, [arrays], core_ids=[0])
    return r.results[0]["out"].reshape(2 * N, N, D)
```

```python
import numpy as np
import concourse.bass as bass
from concourse import mybir
from contextlib import ExitStack

F32 = mybir.dt.float32
ALU = mybir.AluOpType
ACT = mybir.ActivationFunctionType
AX = mybir.AxisListType

N = 64
P = 128
D = 128
STEPS = N - 2
POINTS = 8
PASSES = 6
REFINE = 3
BIG = 1e15

C_ID = 0
C_ONE = C_ID + P
C_LOW = C_ONE + P
C_SEL = C_LOW + N
C_DUP = C_SEL + N
C_PT = C_DUP + P
C_DOWN = C_PT + POINTS
C_J = C_DOWN + N
C_EXP = C_J + 1
C_COLS = C_EXP + 32


def constants():
    c = np.zeros((P, C_COLS), np.float32)
    i = np.arange(P)
    c[:, C_ID:C_ID + P] = np.eye(P)
    c[:, C_ONE:C_ONE + P] = 1
    c[:N, C_LOW:C_LOW + N] = i[:N, None] > i[None, :N]
    c[:N, C_SEL:C_SEL + N] = i[:N, None] == i[None, :N] + 1
    c[:N, C_DUP:C_DUP + P] = i[:N, None] == i[None, :] % N
    c[:, C_PT:C_PT + POINTS] = np.arange(1, POINTS + 1)
    c[:, C_DOWN:C_DOWN + N] = N - np.arange(N)
    c[:, C_J] = i % N
    c[:, C_EXP:C_EXP + 32] = np.tile(8 - np.arange(8), 4)
    return c


class Count:

    def __init__(self, eng, sem):
        self.eng, self.sem, self.n = eng, sem, 0

    def inc(self, ins):
        self.n += 1
        ins.then_inc(self.sem, 1)
        return self.n

    def chain(self, ins):
        self.eng.wait_ge(self.sem, self.inc(ins))
        return self.n


def hold(eng, sem, value):
    eng.wait_ge(sem, value)
    eng.nop(nofuse=True)


def eig_memory(sb, pb):
    m = {}
    for name, shape in dict(
        A=[N, N], AT=[P, N], rowsum=[P, 4], dinv=[P, 4], dd=[P, N], L=[N, N], LT=[N, N],
        Ah=[P, N], tri=[N, N], QT=[N, N], Q=[N, N], X3=[N, 3], S2=[N, 3], c=[N, 8], v=[N, 1],
        rowv=[1, N], rowu=[1, N], H=[N, N], B=[N, N], AI=[N, 2 * N],
        TB=[P, N], EB=[P, N], NE2=[P, N], lim=[P, 8], xs=[P, POINTS],
        TX=[P, N * POINTS], PV=[P, N * POINTS], RC=[P, POINTS], neg=[P, N * POINTS], cnt=[P, POINTS],
        PVC=[P, N], DM=[N, N], g=[N, N], g2=[N, N], onehot=[N, N], rf=[N, N], rb=[N, N], zf=[N, N], zb=[N, N],
        Z=[N, N], ZT=[N, N], sq=[N, N], zc=[N, 8],
        X=[N, N], XT=[N, N], R=[N, N], AX=[N, N], LD=[N, N], den=[N, N], num=[N, N], E0=[N, N], mask=[N, N],
        W=[N, N], sg=[N, 8], sc=[N, 24], UT2=[N, P],
    ).items():
        m[name] = sb("eg_" + name, shape)
    return m


def eig_vector(nc, dve, S, C, m, ps, k1, k2, UB, UTB, AHB):
    V = nc.vector
    own = Count(dve, S("eig_dve"))
    ch = own.chain
    ident = C[0:N, C_ID:C_ID + N]
    low = C[0:N, C_LOW:C_LOW + N]
    sel = C[0:N, C_SEL:C_SEL + N]
    A, AT = m["A"], m["AT"]
    dve.wait_ge(S("const_in"), 16)
    dve.wait_ge(S("adj_in"), 48)
    rs, dinv = m["rowsum"], m["dinv"]
    V.tensor_reduce(rs[0:N, 0:1], A[:, :], AX.X, ALU.add).then_inc(own.sem, 1); own.n += 1
    V.tensor_reduce(rs[0:N, 1:2], AT[0:N, :], AX.X, ALU.add).then_inc(own.sem, 1); own.n += 1
    ch(V.tensor_tensor(m["sq"][:, :], A[:, :], ident, ALU.mult))
    ch(V.tensor_reduce(rs[0:N, 2:3], m["sq"][:, :], AX.X, ALU.add))
    ch(V.tensor_tensor(rs[0:N, 3:4], rs[0:N, 0:1], rs[0:N, 1:2], ALU.add))
    ch(V.tensor_tensor(dinv[0:N, 0:1], rs[0:N, 3:4], rs[0:N, 2:3], ALU.subtract))
    ch(V.tensor_scalar(dinv[0:N, 1:2], dinv[0:N, 0:1], 1.0, None, ALU.add))
    V.tensor_scalar(dinv[0:N, 3:4], dinv[0:N, 0:1], 0.0, None, ALU.is_gt).then_inc(own.sem, 1); own.n += 1
    ch(V.tensor_scalar(dinv[0:N, 2:3], dinv[0:N, 0:1], 1e-30, None, ALU.max))
    V.tensor_copy(m["c"][:, 0:1], dinv[0:N, 2:3]).then_inc(own.sem, 1); own.n += 1
    V.tensor_copy(m["c"][:, 1:2], dinv[0:N, 1:2]).then_inc(S("deg_ready"), 1)
    dve.wait_ge(S("deg_root"), 1)
    ch(V.reciprocal(m["c"][:, 4:6], m["c"][:, 2:4]))
    ch(V.tensor_tensor(m["c"][:, 4:5], m["c"][:, 4:5], dinv[0:N, 3:4], ALU.mult))
    ch(V.tensor_scalar(m["AI"][:, 0:N], ident, m["c"][:, 4:5], None, ALU.mult))
    V.tensor_scalar(m["AI"][:, N:2 * N], ident, m["c"][:, 5:6], None, ALU.mult).then_inc(S("dinv_diag"), 1)
    ch(V.tensor_scalar(m["L"][:, :], ident, dinv[0:N, 0:1], None, ALU.mult))
    ch(V.tensor_tensor(m["L"][:, :], m["L"][:, :], A[:, :], ALU.subtract))
    ch(V.tensor_scalar(m["L"][:, :], m["L"][:, :], m["c"][:, 4:5], None, ALU.mult))
    dve.wait_ge(S("dinv_rows"), 1)
    ch(V.tensor_tensor(m["L"][:, :], m["L"][:, :], ps[0][0:N, 0:N], ALU.mult))
    V.tensor_copy(m["dd"][:, 0:1], ps[0][:, P:P + 1]).then_inc(own.sem, 1); own.n += 1
    ch(V.tensor_tensor(m["Ah"][0:N, :], AT[0:N, :], ident, ALU.add))
    ch(V.tensor_tensor(m["Ah"][N:P, :], AT[N:P, :], C[N:P, C_ID + N:C_ID + P], ALU.add))
    ch(V.tensor_scalar(m["Ah"][:, :], m["Ah"][:, :], m["dd"][:, 0:1], None, ALU.mult))
    ch(V.memset(AHB[:, :], 0.0))
    ch(V.memset(UB[:, :], 0.0))
    ch(V.memset(UTB[:, :], 0.0))
    for h in (0, N):
        ch(V.tensor_tensor(AHB[h:h + N, h:h + N], m["Ah"][h:h + N, :], ps[0][h:h + N, N:2 * N], ALU.mult))
    V.tensor_copy(m["QT"][:, :], ident).then_inc(own.sem, 1); own.n += 1
    V.nop() if False else None
    dve.wait_ge(S("eig_dve"), own.n)
    V.tensor_copy(m["H"][:, :], m["L"][:, :]).then_inc(S("lap_ready"), 1)
    dve.wait_ge(S("lap_turned"), 1)
    ch(V.tensor_tensor(m["L"][:, :], m["L"][:, :], ps[1][0:N, 0:N], ALU.add))
    V.tensor_scalar(m["L"][:, :], m["L"][:, :], 0.5, None, ALU.mult).then_inc(S("lap_sym"), 1)

    hd, hp, ha = S("hh_dve"), S("hh_pe"), S("hh_act")
    ND, NP, NA = 17, 6, 2
    psA, psN, psR, psH, psB = ps[0], ps[1], ps[2], ps[3], ps[4]
    X3, S2, c = m["X3"], m["S2"], m["c"]
    with dve.Fori(0, STEPS) as k:
        b = k * ND

        def step(n, ins, wait=True):
            ins.then_inc(hd, 1)
            if wait:
                dve.wait_ge(hd, b + n)
        hold(dve, hp, k * NP + 1)
        step(1, V.tensor_copy(X3[:, 1:2], sel[:, bass.ds(k, 1)]), False)
        step(2, V.tensor_tensor(X3[:, 2:3], psA[0:N, bass.ds(k, 1)], low[:, bass.ds(k + 1, 1)], ALU.mult), False)
        step(3, V.tensor_tensor(X3[:, 0:1], psA[0:N, bass.ds(k, 1)], low[:, bass.ds(k, 1)], ALU.mult), False)
        dve.wait_ge(hp, k * NP + 2)
        step(4, V.tensor_copy(S2[:, :], psN[0:N, 0:3]), False)
        step(5, V.tensor_scalar(c[:, 0:1], psN[0:N, 1:2], 0.0, 2.0, ALU.is_ge, ALU.mult), False)
        step(6, V.tensor_scalar(c[:, 1:2], psN[0:N, 2:3], 0.0, None, ALU.is_gt))
        dve.wait_ge(ha, k * NA + 1)
        step(7, V.scalar_tensor_tensor(out=c[:, 2:3], in0=c[:, 0:1], scalar=-1.0, in1=c[:, 7:8],
                                       op0=ALU.add, op1=ALU.mult))
        step(8, V.scalar_tensor_tensor(out=m["v"][:, :], in0=X3[:, 1:2], scalar=c[:, 2:3], in1=X3[:, 0:1],
                                       op0=ALU.mult, op1=ALU.add), False)
        step(9, V.scalar_tensor_tensor(out=c[:, 3:4], in0=S2[:, 1:2], scalar=c[:, 2:3], in1=S2[:, 0:1],
                                       op0=ALU.mult, op1=ALU.add))
        step(10, V.tensor_scalar(c[:, 3:4], c[:, 3:4], 1e-36, None, ALU.max))
        step(11, V.reciprocal(c[:, 4:5], c[:, 3:4]))
        step(12, V.tensor_tensor(c[:, 5:6], c[:, 4:5], c[:, 1:2], ALU.mult))
        dve.wait_ge(hp, k * NP + 3)
        step(13, V.tensor_copy(m["rowv"][:, :], psR[0:1, 0:N]), False)
        step(14, V.tensor_scalar(m["rowu"][:, :], psR[0:1, 0:N], c[0:1, 5:6], None, ALU.mult), False)
        dve.wait_ge(hp, k * NP + 4)
        step(15, V.tensor_tensor(m["H"][:, :], ident, psH[0:N, 0:N], ALU.subtract), False)
        dve.wait_ge(hp, k * NP + 5)
        step(16, V.tensor_copy(m["B"][:, :], psB[0:N, 0:N]), False)
        dve.wait_ge(hp, k * NP + 7)
        step(17, V.tensor_copy(m["QT"][:, :], ps[5][0:N, 0:N]), False)

    ch(V.tensor_tensor(m["AI"][:, 0:N], psA[0:N, 0:N], ident, ALU.mult))
    V.tensor_tensor(m["AI"][:, N:2 * N], psA[0:N, 0:N], sel, ALU.mult).then_inc(S("tri_parts"), 1)
    TB, EB, NE2, lim = m["TB"], m["EB"], m["NE2"], m["lim"]
    ch(V.memset(EB[:, :], 0.0))
    dve.wait_ge(S("tri_rows"), 1)
    ch(V.tensor_copy(TB[0:N, :], ps[1][0:N, 0:N]))
    ch(V.tensor_copy(TB[N:P, :], ps[1][N:P, 0:N][:, ::-1]))
    ch(V.tensor_copy(EB[0:N, 0:N - 1], ps[1][0:N, N:2 * N - 1]))
    ch(V.tensor_copy(EB[N:P, 0:N - 1], ps[1][N:P, N:2 * N - 1][:, ::-1]))
    ch(V.tensor_tensor(NE2[:, :], EB[:, :], EB[:, :], ALU.mult))
    ch(V.tensor_scalar(NE2[:, :], NE2[:, :], 1e-30, -1.0, ALU.max, ALU.mult))
    ch(V.tensor_reduce(lim[:, 0:1], TB[:, :], AX.X, ALU.max, apply_absolute_value=True))
    ch(V.tensor_reduce(lim[:, 1:2], EB[:, :], AX.X, ALU.max, apply_absolute_value=True))
    ch(V.scalar_tensor_tensor(out=lim[:, 2:3], in0=lim[:, 1:2], scalar=2.0, in1=lim[:, 0:1],
                              op0=ALU.mult, op1=ALU.add))
    ch(V.tensor_scalar(lim[:, 2:3], lim[:, 2:3], 1.001, 1e-20, ALU.mult, ALU.add))
    ch(V.tensor_scalar(lim[:, 3:4], lim[:, 2:3], -1.0, None, ALU.mult))
    ch(V.tensor_scalar(lim[:, 4:5], lim[:, 2:3], 2.0 / (POINTS + 1), None, ALU.mult))

    TX = m["TX"][:, :].rearrange("p (i q) -> p i q", i=N)
    PV = m["PV"][:, :].rearrange("p (i q) -> p i q", i=N)
    RC = m["RC"]

    def pivots(link, q):
        link(V.tensor_tensor(TX[:, :, 0:q], TB[:, :].unsqueeze(2).to_broadcast([P, N, q]),
                             m["xs"][:, 0:q].unsqueeze(1).to_broadcast([P, N, q]), ALU.subtract))
        link(V.tensor_copy(PV[:, 0, 0:q], TX[:, 0, 0:q]))
        for i in range(1, N):
            link(V.reciprocal(RC[:, 0:q], PV[:, i - 1, 0:q]))
            link(V.scalar_tensor_tensor(out=PV[:, i, 0:q], in0=RC[:, 0:q], scalar=NE2[:, i - 1:i],
                                        in1=TX[:, i, 0:q], op0=ALU.mult, op1=ALU.add))

    sect = S("sect_dve")
    PER = 2 + 2 * (N - 1) + 6
    with dve.Fori(0, PASSES) as p:
        at = [0]

        def link(ins):
            at[0] += 1
            ins.then_inc(sect, 1)
            dve.wait_ge(sect, p * PER + at[0])
        link(V.tensor_scalar(m["xs"][:, :], C[:, C_PT:C_PT + POINTS], lim[:, 4:5], lim[:, 3:4], ALU.mult, ALU.add))
        pivots(link, POINTS)
        link(V.tensor_scalar(m["neg"][:, :], m["PV"][:, :], 0.0, None, ALU.is_lt))
        link(V.tensor_reduce(m["cnt"][:, :], m["neg"][:, :].rearrange("p (i q) -> p q i", i=N), AX.X, ALU.add))
        link(V.tensor_scalar(RC[:, :], m["cnt"][:, :], C[:, C_J:C_J + 1], None, ALU.is_le, ALU.add,
                             accum_out=lim[:, 5:6]))
        link(V.scalar_tensor_tensor(out=lim[:, 3:4], in0=lim[:, 5:6], scalar=lim[:, 4:5], in1=lim[:, 3:4],
                                    op0=ALU.mult, op1=ALU.add))
        link(V.tensor_scalar(lim[:, 4:5], lim[:, 4:5], 1.0 / (POINTS + 1), None, ALU.mult))
        assert at[0] == PER, at
    ch(V.scalar_tensor_tensor(out=lim[:, 6:7], in0=lim[:, 4:5], scalar=0.5 * (POINTS + 1), in1=lim[:, 3:4],
                              op0=ALU.mult, op1=ALU.add))
    V.tensor_copy(lim[:, 7:8], lim[:, 6:7]).then_inc(S("lam_ready"), 1)
    dve.wait_ge(S("lam_both"), 1)
    ch(V.tensor_copy(m["xs"][:, 0:1], ps[2][:, 0:1]))
    pivots(ch, 1)
    ch(V.tensor_scalar(m["PVC"][:, :], PV[:, :, 0], BIG, -BIG, ALU.min, ALU.max))
    V.tensor_copy(m["PVC"][:, 0:1], m["PVC"][:, 0:1]).then_inc(S("pivots_ready"), 1)
    dve.wait_ge(S("pivots_moved"), 1)
    DF, DM = m["PVC"][0:N, :], m["DM"]
    ch(V.tensor_copy(DM[:, :], ps[3][0:N, 0:N][:, ::-1]))
    g, g2, oh = m["g"], m["g2"], m["onehot"]
    ch(V.tensor_tensor(g[:, :], DM[:, :], DF, ALU.add))
    ch(V.tensor_tensor(g[:, :], g[:, :], TX[0:N, :, 0], ALU.subtract))
    ch(V.tensor_tensor(g[:, :], g[:, :], g[:, :], ALU.mult))
    ch(V.tensor_reduce(m["zc"][:, 0:1], g[:, :], AX.X, ALU.min))
    ch(V.scalar_tensor_tensor(out=g2[:, :], in0=g[:, :], scalar=m["zc"][:, 0:1], in1=C[0:N, C_DOWN:C_DOWN + N],
                              op0=ALU.is_le, op1=ALU.mult))
    ch(V.tensor_reduce(m["zc"][:, 1:2], g2[:, :], AX.X, ALU.max))
    ch(V.tensor_scalar(oh[:, :], g2[:, :], m["zc"][:, 1:2], None, ALU.is_equal))
    for r, d in ((m["rf"], DF), (m["rb"], DM[:, :])):
        ch(V.reciprocal(r[:, :], d))
        ch(V.tensor_scalar(r[:, :], r[:, :], 1e18, -1e18, ALU.min, ALU.max))
        ch(V.tensor_scalar(r[:, :], r[:, :], -1.0, None, ALU.mult))
    ch(V.tensor_tensor(m["rf"][:, 0:N], m["rf"][:, 0:N], EB[0:N, 0:N], ALU.mult))
    ch(V.tensor_tensor(m["rb"][:, 1:N], m["rb"][:, 1:N], EB[0:N, 0:N - 1], ALU.mult))
    ch(V.memset(m["rb"][:, 0:1], 0.0))
    ch(V.tensor_tensor_scan(m["zf"][:, :], m["rb"][:, :], oh[:, :], 0.0, ALU.mult, ALU.add))
    ch(V.tensor_tensor_scan(m["zb"][:, :][:, ::-1], m["rf"][:, :][:, ::-1], oh[:, :][:, ::-1], 0.0, ALU.mult, ALU.add))
    Z = m["Z"]
    ch(V.tensor_tensor(Z[:, :], m["zf"][:, :], m["zb"][:, :], ALU.add))
    ch(V.tensor_tensor(Z[:, :], Z[:, :], oh[:, :], ALU.subtract))
    ch(V.tensor_scalar(Z[:, :], Z[:, :], 1e15, -1e15, ALU.min, ALU.max))
    V.scalar_tensor_tensor(out=m["sq"][:, :], in0=Z[:, :], scalar=1.0, in1=Z[:, :], op0=ALU.mult, op1=ALU.mult,
                           accum_out=m["zc"][:, 2:3]).then_inc(S("znorm2"), 1)
    dve.wait_ge(S("znorm"), 1)
    ch(V.reciprocal(m["zc"][:, 4:5], m["zc"][:, 3:4]))
    V.tensor_scalar(Z[:, :], Z[:, :], m["zc"][:, 4:5], None, ALU.mult).then_inc(S("z_ready"), 1)
    dve.wait_ge(S("z_turned"), 1)
    V.tensor_copy(m["ZT"][:, :], ps[4][0:N, 0:N]).then_inc(S("zt_ready"), 1)
    dve.wait_ge(S("u_first"), 1)
    V.tensor_copy(m["Q"][:, :], ps[6][0:N, 0:N]).then_inc(own.sem, 1); own.n += 1
    V.tensor_copy(m["XT"][:, :], ps[6][0:N, N:2 * N]).then_inc(own.sem, 1); own.n += 1
    V.tensor_copy(m["X"][:, :], ps[5][0:N, 0:N]).then_inc(S("x_ready"), 1)

    R, zc = m["R"], m["zc"]
    for r in range(REFINE):
        dve.wait_ge(S("gram_ready"), r + 1)
        V.tensor_copy(m["AX"][:, :], ps[1][0:N, 0:N]).then_inc(S("ax_ready"), 1)
        ch(V.tensor_tensor(R[:, :], ident, ps[0][0:N, 0:N], ALU.subtract))
        ch(V.tensor_tensor(m["sq"][:, :], ident, ps[0][0:N, 0:N], ALU.mult))
        ch(V.tensor_reduce(zc[:, 5:6], m["sq"][:, :], AX.X, ALU.add))
        ch(V.reciprocal(zc[:, 5:6], zc[:, 5:6]))
        dve.wait_ge(S("s_ready"), r + 1)
        ch(V.tensor_tensor(m["sq"][:, :], ident, ps[2][0:N, 0:N], ALU.mult))
        ch(V.tensor_reduce(zc[:, 6:7], m["sq"][:, :], AX.X, ALU.add))
        ch(V.tensor_tensor(zc[:, 7:8], zc[:, 6:7], zc[:, 5:6], ALU.mult))
        V.tensor_scalar(m["LD"][:, :], ident, zc[:, 7:8], None, ALU.mult).then_inc(S("lamdiag_ready"), 1)
        dve.wait_ge(S("lamrow_ready"), r + 1)
        ch(V.tensor_scalar(m["den"][:, :], ps[3][0:N, 0:N], zc[:, 7:8], None, ALU.subtract))
        ch(V.tensor_tensor(m["num"][:, :], R[:, :], ps[3][0:N, 0:N], ALU.mult))
        ch(V.tensor_tensor(m["num"][:, :], m["num"][:, :], ps[2][0:N, 0:N], ALU.add))
        ch(V.tensor_scalar(m["mask"][:, :], m["den"][:, :], 0.0, 1.0 / BIG, ALU.is_equal, ALU.mult))
        ch(V.tensor_tensor(m["den"][:, :], m["den"][:, :], m["mask"][:, :], ALU.add))
        ch(V.reciprocal(m["den"][:, :], m["den"][:, :]))
        ch(V.tensor_scalar(m["den"][:, :], m["den"][:, :], BIG, -BIG, ALU.min, ALU.max))
        ch(V.tensor_tensor(m["E0"][:, :], m["num"][:, :], m["den"][:, :], ALU.mult))
        ch(V.tensor_tensor(m["mask"][:, :], m["E0"][:, :], m["E0"][:, :], ALU.mult))
        ch(V.tensor_scalar(m["mask"][:, :], m["mask"][:, :], 0.25, None, ALU.is_le))
        ch(V.tensor_tensor(m["E0"][:, :], m["E0"][:, :], m["mask"][:, :], ALU.mult))
        ch(V.tensor_scalar(R[:, :], R[:, :], 0.5, None, ALU.mult))
        ch(V.tensor_scalar(m["mask"][:, :], m["mask"][:, :], -1.0, 1.0, ALU.mult, ALU.add))
        ch(V.tensor_tensor(R[:, :], R[:, :], m["mask"][:, :], ALU.mult))
        ch(V.tensor_tensor(R[:, :], R[:, :], m["E0"][:, :], ALU.add))
        V.tensor_tensor(m["LD"][:, :], R[:, :], ident, ALU.add).then_inc(S("e_ready"), 1)
        dve.wait_ge(S("x_next"), r + 1)
        V.tensor_copy(m["XT"][:, :], ps[4][0:N, N:2 * N]).then_inc(own.sem, 1); own.n += 1
        V.tensor_copy(m["X"][:, :], ps[4][0:N, 0:N]).then_inc(S("x_ready"), 1)

    W, sc, sg = m["W"], m["sc"], m["sg"]
    dve.wait_ge(S("w_ready"), 1)
    ch(V.tensor_copy(W[:, :], ps[0][0:N, 0:N]))
    for a, cut in enumerate((31, 15, 47)):
        ch(V.tensor_scalar(sg[:, a:a + 1], EB[0:N, cut:cut + 1], 0.0, 2.0, ALU.is_ge, ALU.mult))
        ch(V.tensor_scalar(sg[:, a:a + 1], sg[:, a:a + 1], -1.0, None, ALU.add))
        ch(V.scalar_tensor_tensor(out=sc[:, a:a + 1], in0=W[:, cut + 1:cut + 2], scalar=sg[:, a:a + 1],
                                  in1=W[:, cut:cut + 1], op0=ALU.mult, op1=ALU.add))
    ch(V.tensor_tensor(sc[:, 3:4], sc[:, 0:1], EB[0:N, 31:32], ALU.mult))
    ch(V.tensor_tensor(sc[:, 3:4], sc[:, 3:4], sc[:, 3:4], ALU.mult))
    ch(V.tensor_tensor(sc[:, 4:5], m["lim"][0:N, 0:1], m["lim"][0:N, 1:2], ALU.max))
    ch(V.tensor_scalar(sc[:, 4:5], sc[:, 4:5], 7e-7 / 2 ** 0.5, None, ALU.mult))
    ch(V.tensor_tensor(sc[:, 4:5], sc[:, 4:5], sc[:, 4:5], ALU.mult))
    ch(V.tensor_tensor(sc[:, 5:6], sc[:, 3:4], sc[:, 4:5], ALU.is_gt))
    ch(V.scalar_tensor_tensor(out=m["sq"][:, 0:N // 2], in0=W[:, 0:N // 2], scalar=1.0, in1=W[:, 0:N // 2],
                              op0=ALU.mult, op1=ALU.mult, accum_out=sc[:, 6:7]))
    ch(V.tensor_scalar(sc[:, 7:8], sc[:, 6:7], 0.5, None, ALU.is_gt))
    for into, mask, yes, no in ((8, 7, 1, 2), (12, 5, 0, 8)):
        ch(V.tensor_scalar(sc[:, into + 1:into + 2], sc[:, mask:mask + 1], -1.0, 1.0, ALU.mult, ALU.add))
        ch(V.tensor_tensor(sc[:, into + 2:into + 3], sc[:, mask:mask + 1], sc[:, yes:yes + 1], ALU.mult))
        ch(V.tensor_tensor(sc[:, into + 1:into + 2], sc[:, into + 1:into + 2], sc[:, no:no + 1], ALU.mult))
        ch(V.tensor_tensor(sc[:, into:into + 1], sc[:, into + 1:into + 2], sc[:, into + 2:into + 3], ALU.add))
    ch(V.tensor_scalar(sc[:, 16:17], sc[:, 12:13], 0.0, 2.0, ALU.is_lt, ALU.mult))
    ch(V.tensor_scalar(sc[:, 17:18], sc[:, 16:17], -1.0, None, ALU.add))
    ch(V.tensor_scalar(m["UT2"][:, 0:N], m["XT"][:, :], sc[:, 17:18], None, ALU.mult))
    V.tensor_scalar(m["UT2"][:, N:P], m["XT"][:, :], sc[:, 17:18], None, ALU.mult).then_inc(S("ut_ready"), 1)
    dve.wait_ge(S("blocks_ready"), 1)
    for h in (0, N):
        ch(V.tensor_copy(UB[h:h + N, h:h + N], ps[1][h:h + N, 0:N]))
        ch(V.tensor_copy(UTB[h:h + N, h:h + N], ps[1][h:h + N, N:2 * N]))


def eig_tensor(nc, pe, S, C, m, ps):
    T = nc.tensor
    ident, ones = C[0:N, C_ID:C_ID + N], C[0:N, C_ONE:C_ONE + P]

    def mm(out, lhsT, rhs):
        return T.matmul(out, lhsT, rhs, start=True, stop=True)
    pe.wait_ge(S("const_in"), 16)
    pe.wait_ge(S("dinv_diag"), 1)
    pe.wait_ge(S("eig_dve"), 1)
    mm(ps[0][:, 0:P], ones, m["AI"][:, :])
    mm(ps[0][:, P:P + 1], C[0:N, C_DUP:C_DUP + P], m["c"][:, 5:6]).then_inc(S("dinv_rows"), 1)
    pe.wait_ge(S("lap_ready"), 1)
    T.transpose(ps[1][0:N, 0:N], m["H"][:, :], ident).then_inc(S("lap_turned"), 1)
    pe.wait_ge(S("lap_sym"), 1)
    T.transpose(ps[0][0:N, 0:N], m["L"][:, :], ident).then_inc(S("hh_pe"), 1)
    hd, hp, ha = S("hh_dve"), S("hh_pe"), S("hh_act")
    ND, NP, NA = 17, 6, 2
    with pe.Fori(0, STEPS) as k:
        b = k * ND
        hold(pe, hd, b + 3)
        mm(ps[1][0:N, 0:3], m["X3"][:, 0:1].to_broadcast([N, N]), m["X3"][:, 0:3]).then_inc(hp, 1)
        hold(pe, hd, b + 8)
        mm(ps[2][0:1, 0:N], m["v"][:, :], ident).then_inc(hp, 1)
        hold(pe, hd, b + 14)
        mm(ps[3][0:N, 0:N], m["rowv"][:, :], m["rowu"][:, :]).then_inc(hp, 1)
        hold(pe, hd, b + 15)
        hold(pe, ha, k * NA + 2)
        mm(ps[4][0:N, 0:N], m["tri"][:, :], m["H"][:, :]).then_inc(hp, 1)
        hold(pe, hd, b + 16)
        mm(ps[0][0:N, 0:N], m["H"][:, :], m["B"][:, :]).then_inc(hp, 1)
        mm(ps[5][0:N, 0:N], m["H"][:, :], m["QT"][:, :]).then_inc(hp, 1)
    pe.wait_ge(S("tri_parts"), 1)
    mm(ps[1][:, 0:P], ones, m["AI"][:, :]).then_inc(S("tri_rows"), 1)
    pe.wait_ge(S("lam_ready"), 1)
    mm(ps[2][:, 0:1], C[0:N, C_DUP:C_DUP + P], m["lim"][0:N, 6:7]).then_inc(S("lam_both"), 1)
    pe.wait_ge(S("pivots_ready"), 1)
    mm(ps[3][0:N, 0:N], C[:, C_ID + N:C_ID + P], m["PVC"][:, :]).then_inc(S("pivots_moved"), 1)
    pe.wait_ge(S("z_ready"), 1)
    T.transpose(ps[4][0:N, 0:N], m["Z"][:, :], ident).then_inc(S("z_turned"), 1)
    T.transpose(ps[6][0:N, 0:N], m["QT"][:, :], ident)
    pe.wait_ge(S("zt_ready"), 1)
    mm(ps[6][0:N, N:2 * N], m["ZT"][:, :], m["QT"][:, :])
    mm(ps[5][0:N, 0:N], m["QT"][:, :], m["ZT"][:, :]).then_inc(S("u_first"), 1)
    for r in range(REFINE):
        pe.wait_ge(S("x_ready"), r + 1)
        mm(ps[1][0:N, 0:N], m["L"][:, :], m["X"][:, :])
        mm(ps[0][0:N, 0:N], m["X"][:, :], m["X"][:, :]).then_inc(S("gram_ready"), 1)
        pe.wait_ge(S("ax_ready"), r + 1)
        mm(ps[2][0:N, 0:N], m["X"][:, :], m["AX"][:, :]).then_inc(S("s_ready"), 1)
        pe.wait_ge(S("lamdiag_ready"), r + 1)
        mm(ps[3][0:N, 0:N], ones[:, 0:N], m["LD"][:, :]).then_inc(S("lamrow_ready"), 1)
        pe.wait_ge(S("e_ready"), r + 1)
        mm(ps[4][0:N, N:2 * N], m["LD"][:, :], m["XT"][:, :])
        mm(ps[4][0:N, 0:N], m["XT"][:, :], m["LD"][:, :]).then_inc(S("x_next"), 1)
    pe.wait_ge(S("x_ready"), REFINE + 1)
    mm(ps[0][0:N, 0:N], m["X"][:, :], m["Q"][:, :]).then_inc(S("w_ready"), 1)
    pe.wait_ge(S("ut_ready"), 1)
    mm(ps[1][:, 0:N], m["UT2"][:, :], ident)
    mm(ps[1][:, N:2 * N], C[0:N, C_DUP:C_DUP + P], m["UT2"][:, 0:N]).then_inc(S("blocks_ready"), 1)


def eig_scalar(nc, act, S, m, ps):
    act.wait_ge(S("deg_ready"), 1)
    act.wait_ge(S("eig_dve"), 1)
    nc.scalar.activation(m["c"][:, 2:4], m["c"][:, 0:2], ACT.Sqrt).then_inc(S("deg_root"), 1)
    hd, ha = S("hh_dve"), S("hh_act")
    act.wait_ge(S("hh_pe"), 1)
    act.wait_ge(S("dinv_rows"), 1)
    with act.Fori(0, STEPS) as k:
        act.wait_ge(hd, k * 17 + 4)
        nc.scalar.activation(m["c"][:, 7:8], m["S2"][:, 0:1], ACT.Sqrt).then_inc(ha, 1)
        nc.scalar.copy(m["tri"][:, :], ps[0][0:N, 0:N]).then_inc(ha, 1)
    act.wait_ge(S("znorm2"), 1)
    nc.scalar.activation(m["zc"][:, 3:4], m["zc"][:, 2:3], ACT.Sqrt).then_inc(S("znorm"), 1)



TILES = 16
PAIRS = 4
TOK = PAIRS * P
E8 = 8
HID0 = 341
CH0 = [(0, 128), (128, 128), (256, 85)]
CH1 = 4
EPS = 1e-5


def ln_stats(V, dv, t, w, x):
    for q in range(PAIRS):
        V.bn_stats(t["bn"][:, w, q, :], x(q)).then_inc(dv, 1)


def ln_sums(V, dv, t, w):
    for q in range(PAIRS):
        V.bn_aggr(t["mv"][:, w, q, :], t["bn"][:, w, q, :]).then_inc(dv, 1)


def ln_var(V, dv, t, w):
    V.tensor_scalar(t["sd"][:, w, 0:PAIRS], t["mv"][:, w, :, 1], EPS, None, ALU.add).then_inc(dv, 1)


def ln_root(A, ac, t, w):
    A.activation(t["sd"][:, w, 4:4 + PAIRS], t["sd"][:, w, 0:PAIRS], ACT.Sqrt).then_inc(ac, 1)


def ln_inverse(V, dv, t, w):
    V.reciprocal(t["sd"][:, w, 8:8 + PAIRS], t["sd"][:, w, 4:4 + PAIRS]).then_inc(dv, 1)


def ln_apply(V, dv, t, w, x, xh):
    for q in range(PAIRS):
        ins = V.tensor_scalar(xh[:, q, :], x(q), t["mv"][:, w, q, 0:1], t["sd"][:, w, 8 + q:9 + q],
                              ALU.subtract, ALU.mult)
    ins.then_inc(dv, 1)


def pairs(ap):
    return ap.rearrange("p (q d) -> p q d", q=PAIRS)


def stage_gnn0(nc, eng, who, S, C, t, ps):
    X, XT = t["X"], t["xT"]
    ident = C[:, C_ID:C_ID + P]
    WAYS = 4
    ND, NP, NA = 24, 5, 5
    ways = range(WAYS)
    dv, pe_s, ac = ([S(f"g0_{n}{w}") for w in ways] for n in ("dve", "pe", "act"))
    xh, ga, gh, gm = (t["way"][k] for k in ("xh", "ga", "gh", "gm"))
    with eng.Fori(0, TILES // WAYS) as i:
        def after(sem, per, n):
            hold(eng, sem, i * per + n)

        def x(w):
            return lambda q: X[:, bass.ds(i * (WAYS * PAIRS) + (w * PAIRS + q), 1), :].rearrange("p o d -> p (o d)")

        def xt(w):
            return X[:, bass.ds(i * (WAYS * PAIRS) + w * PAIRS, PAIRS), :]
        if who == "dve":
            V = nc.vector
            for w in ways:
                ln_stats(V, dv[w], t, w, x(w))
            for w in ways:
                after(dv[w], ND, 4)
                ln_sums(V, dv[w], t, w)
            for w in ways:
                after(dv[w], ND, 8)
                ln_var(V, dv[w], t, w)
            for w in ways:
                after(ac[w], NA, 1)
                ln_inverse(V, dv[w], t, w)
            for w in ways:
                after(dv[w], ND, 10)
                ln_apply(V, dv[w], t, w, x(w), xh[w])
            for w in ways:
                after(pe_s[w], NP, 3)
                V.tensor_tensor(gm[w][:, :], ps[2 * w][:, :], t["b2row"][:, :], ALU.add).then_inc(dv[w], 1)
            for w in ways:
                after(pe_s[w], NP, 4)
                V.tensor_tensor(xt(w), xt(w), pairs(ps[2 * w + 1][:, :]), ALU.add).then_inc(dv[w], 1)
            for w in ways:
                after(dv[w], ND, 13)
                ln_stats(V, dv[w], t, w, x(w))
            for w in ways:
                after(dv[w], ND, 17)
                ln_sums(V, dv[w], t, w)
            for w in ways:
                after(dv[w], ND, 21)
                ln_var(V, dv[w], t, w)
            for w in ways:
                after(ac[w], NA, 4)
                ln_inverse(V, dv[w], t, w)
            for w in ways:
                after(dv[w], ND, 23)
                ln_apply(V, dv[w], t, w, x(w), xh[w])
        if who == "pe":
            T = nc.tensor
            for w in ways:
                after(dv[w], ND, 11)
                for q in range(PAIRS):
                    ins = T.matmul(ps[2 * w][:, q * P:(q + 1) * P], xh[w][:, q, :], t["UB"][:, :], start=True, stop=True)
                ins.then_inc(pe_s[w], 1)
            for w in ways:
                after(ac[w], NA, 2)
                T.matmul(ps[2 * w + 1][:, :], t["w1g0"][:, :], ga[w][:, :], start=True, stop=True).then_inc(pe_s[w], 1)
            for w in ways:
                after(ac[w], NA, 3)
                for q in range(PAIRS):
                    ins = T.matmul(ps[2 * w][:, q * P:(q + 1) * P], gh[w][:, q * P:(q + 1) * P], t["w2g0"][:, :],
                                   start=True, stop=True)
                ins.then_inc(pe_s[w], 1)
            for w in ways:
                after(dv[w], ND, 12)
                T.matmul(ps[2 * w + 1][:, :], t["UTB"][:, :], gm[w][:, :], start=True, stop=True).then_inc(pe_s[w], 1)
            for w in ways:
                after(dv[w], ND, 24)
                for q in range(PAIRS):
                    ins = T.transpose(ps[2 * w][:, q * P:(q + 1) * P], xh[w][:, q, :], ident)
                ins.then_inc(pe_s[w], 1)
        if who == "act":
            A = nc.scalar
            for w in ways:
                after(dv[w], ND, 9)
                ln_root(A, ac[w], t, w)
            for w in ways:
                after(pe_s[w], NP, 1)
                A.copy(ga[w][:, :], ps[2 * w][:, :]).then_inc(ac[w], 1)
            for w in ways:
                after(pe_s[w], NP, 2)
                A.activation(gh[w][:, :], ps[2 * w + 1][:, :], ACT.Relu, bias=t["b1g0"][:, 0:1]).then_inc(ac[w], 1)
            for w in ways:
                after(dv[w], ND, 22)
                ln_root(A, ac[w], t, w)
            for w in ways:
                after(pe_s[w], NP, 5)
                A.copy(XT[:, bass.ds(i * (WAYS * TOK) + w * TOK, TOK)], ps[2 * w][:, :]).then_inc(ac[w], 1)


class Route:

    ND = 24

    def __init__(self, nc, eng, S, C, t, bank, layer, tile, wait):
        self.nc, self.eng, self.C, self.t, self.bank, self.layer, self.tile, self.wait = nc, eng, C, t, bank, layer, tile, wait
        self.s = lambda n: S(f"r{layer}_{n}")
        self.a, self.b, self.o1, self.o2, self.sc = (t["rt"][:, k, :] for k in range(5))

    def after(self, name, per, n):
        self.wait(self.eng, self.s(name), self.tile * per + n)

    def fetch(self):
        self.after("read", 1, 1)
        self.nc.gpsimd.tensor_copy(self.t["xr"][:, :], self.t["xT"][:, bass.ds(self.tile * TOK, TOK)]
                                   ).then_inc(self.s("fetched"), 1)

    def logits(self):
        self.after("fetched", 1, 1)
        for q in range(PAIRS):
            ins = self.nc.tensor.matmul(self.bank[:, q * E8:(q + 1) * E8], self.t["xr"][:, q * P:(q + 1) * P],
                                        self.t[f"wr{self.layer}"][:, :], start=True, stop=True)
        ins.then_inc(self.s("read"), 1)

    def views(self):
        V, at, dv = self.nc.vector, [0], self.s("dve")
        v = lambda x: x.rearrange("p (q e) -> p q e", q=PAIRS)
        cols = lambda k: self.t["rc"][:, k, :]
        wide = lambda k: cols(k).unsqueeze(2).to_broadcast([P, PAIRS, E8])

        def go(ins, n):
            ins.then_inc(dv, 1)
            self.after("dve", self.ND, n)
        return V, v, cols, wide, go

    def shifted(self):
        V, v, cols, wide, go = self.views()
        self.after("read", 1, 2)
        go(V.tensor_copy(self.a, self.bank[:, 0:PAIRS * E8]), 1)
        go(V.tensor_reduce(cols(0), v(self.a), AX.X, ALU.max), 2)
        go(V.tensor_tensor(v(self.a), v(self.a), wide(0), ALU.subtract), 3)

    def exp(self):
        self.after("dve", self.ND, 3)
        self.nc.scalar.activation(self.b, self.a, ACT.Exp).then_inc(self.s("exp"), 1)

    def choose(self):
        V, v, cols, wide, go = self.views()
        a, b, o1, o2, sc = self.a, self.b, self.o1, self.o2, self.sc
        self.after("exp", 1, 1)
        go(V.tensor_reduce(cols(1), v(b), AX.X, ALU.add), 4)
        go(V.reciprocal(cols(2), cols(1)), 5)
        go(V.tensor_tensor(v(b), v(b), wide(2), ALU.mult), 6)
        n = 6
        for o, src in ((o1, b), (o2, a)):
            go(V.tensor_reduce(cols(3), v(src), AX.X, ALU.max), n + 1)
            go(V.tensor_tensor(v(o), v(src), wide(3), ALU.is_equal), n + 2)
            go(V.tensor_tensor(sc, o, self.C[:, C_EXP:C_EXP + PAIRS * E8], ALU.mult), n + 3)
            go(V.tensor_reduce(cols(4), v(sc), AX.X, ALU.max), n + 4)
            go(V.tensor_tensor(v(o), v(sc), wide(4), ALU.is_equal), n + 5)
            n += 5
            if o is o1:
                go(V.scalar_tensor_tensor(out=a, in0=o1, scalar=-2.0, in1=b, op0=ALU.mult, op1=ALU.add), n + 1)
                n += 1
        go(V.tensor_tensor(o1, o1, o2, ALU.add), 18)
        go(V.tensor_tensor(b, b, o1, ALU.mult), 19)
        go(V.tensor_reduce(cols(5), v(b), AX.X, ALU.add), 20)
        go(V.tensor_scalar(cols(5), cols(5), 1e-9 if self.layer == 0 else 0.0, None, ALU.add), 21)
        go(V.reciprocal(cols(6), cols(5)), 22)
        go(V.tensor_tensor(v(b), v(b), wide(6), ALU.mult), 23)

    def turn(self):
        self.after("dve", self.ND, 23)
        for q in range(PAIRS):
            ins = self.nc.tensor.transpose(self.bank[0:E8, q * P:(q + 1) * P], self.b[:, q * E8:(q + 1) * E8],
                                           self.C[:, C_ID:C_ID + P])
        ins.then_inc(self.s("turned"), 1)

    def keep(self):
        self.after("turned", 1, 1)
        self.after("gates_out", 16, 1)
        self.nc.vector.tensor_copy(self.t["gT"][:, :], self.bank[0:E8, :]).then_inc(self.s("dve"), 1)

    def store(self):
        self.after("dve", self.ND, 24)
        self.eng.dma_start(self.t[f"gates{self.layer}"][:, bass.ds(self.tile * TOK, TOK)], self.t["gT"][:, :]
                           ).then_inc(self.s("gates_out"), 16)
        self.after("gates_out", 16, 17)

    def begin(self, who):
        if who == "pe":
            self.eng.sem_inc(self.s("read"), 1)
        if who == "sp":
            self.eng.sem_inc(self.s("gates_out"), 1)


def stage_experts(nc, eng, who, S, C, t, ps, layer, out=None):
    X, XT = t["X"], t["xT"]
    ident = C[:, C_ID:C_ID + P]
    s = lambda n: S(f"f{layer}_{n}")
    units = [(e, c) for e in range(E8) for c in range(3)] if layer == 0 else \
            [(e, c) for e in range(E8 + 1) for c in range(CH1)]
    NU = len(units)
    GB = t["GB"]
    NB = 2 if layer == 0 else 3
    HALF = TILES // 2

    SEEDED = NU + 1
    if who == "dve":
        for n in ("gated", "y_added"):
            eng.sem_inc(s(n), SEEDED)
    if who == "act":
        eng.sem_inc(s("act"), SEEDED)
    if who == "pe":
        eng.sem_inc(s("down"), SEEDED)
        eng.sem_inc(s("y_sum"), SEEDED)
    if who == "pool":
        eng.sem_inc(s("xo_free"), SEEDED)
    SEED = {s(n).name: SEEDED for n in ("gated", "y_added", "act", "down", "y_sum", "xo_free")}

    def static(eng, sem, value):
        eng.wait_ge(sem, value)

    def gate_rows(dst_par, col):
        for e in range(E8):
            eng.dma_start(GB[:, dst_par, e, :], t[f"gates{layer}"][e:e + 1, col].to_broadcast([P, TOK])
                          ).then_inc(S(f"f{layer}_gates{dst_par}"), 16)
        if layer == 1:
            eng.dma_start(t["g9"][:, dst_par, :], t["gates1"][:, col]).then_inc(S(f"f1_gates{dst_par}"), 16)

    first = Route(nc, eng, S, C, t, ps[7], layer, 0, static)
    first.begin(who)
    if who == "pool":
        first.fetch()
    if who == "pe":
        first.logits()
        first.turn()
    if who == "act":
        first.exp()
    if who == "dve":
        first.shifted()
        first.choose()
        first.keep()
    if who == "sp":
        first.store()
        gate_rows(0, slice(0, TOK))

    def wide_of(u):
        return CH0[units[u][1]][1] if layer == 0 else P
    with eng.Fori(0, HALF) as it:
        for par in range(2):
            tile = it * 2 + par
            tk = bass.ds(it * (2 * TOK) + par * TOK, TOK)

            def after(sem, per, n, par=par):
                hold(eng, sem, it * (2 * per) + (par * per + n + SEED.get(sem.name, 0)))
            nxt = Route(nc, eng, S, C, t, ps[7 - par], layer, it * 2 + (par + 1), hold)
            if who == "pool":
                nxt.fetch()
            if who == "sp":
                nxt.store()
                after(s("gated"), NU, 0)
                if layer == 1:
                    after(s("y_sum"), 1, 0)
                gate_rows(1 - par, bass.ds(it * (2 * TOK) + (par + 1) * TOK, TOK))
            NG = E8 + layer
            if who == "pe":
                T = nc.tensor
                y = ps[4 + par]

                def up(u):
                    e, c = units[u]
                    w = wide_of(u)
                    if layer == 0:
                        after(s("gated"), NU, u - 1)
                        T.matmul(ps[u % 2][0:w, :], t["w1f0"][:, e, CH0[c][0]:CH0[c][0] + w], XT[:, tk],
                                 start=True, stop=True)
                        T.matmul(ps[2 + u % 2][0:w, :], t["w3f0"][:, e, CH0[c][0]:CH0[c][0] + w], XT[:, tk],
                                 start=True, stop=True).then_inc(s("up"), 1)
                    else:
                        after(s("act"), NU, u - 3)
                        T.matmul(ps[u % 4][:, :], t["w1f1"][:, e, c * P:(c + 1) * P], XT[:, tk],
                                 start=True, stop=True).then_inc(s("up"), 1)

                def down(u):
                    e, c = units[u]
                    w = wide_of(u)
                    after(s("gated"), NU, u + 1)
                    src = t["hg"][:, u % 4, :]
                    wt = t[f"w2f{layer}"]
                    last = layer == 0 and u == NU - 1
                    ins = T.matmul(y[:, :], wt[0:w, e, c, :], src[0:w, :], start=(u == 0), stop=last,
                                   skip_group_check=True)
                    ins.then_inc(s("down"), 1)
                    return ins
                for u in range(NU + 1):
                    if u == 3:
                        after(s("y_added"), 1, 0)
                        nxt.logits()
                    if u == 14:
                        nxt.turn()
                    if u < NU:
                        up(u)
                    if u >= 1:
                        down(u - 1)
                if layer == 1:
                    hold(eng, S(f"f1_gates{par}"), it * (16 * NG) + 16 * NG)
                    T.matmul(y[:, :], t["b2p"][:, :], t["g9"][:, par, :], start=False, stop=True,
                             skip_group_check=True).then_inc(s("y_sum"), 1)
                else:
                    T.nop().then_inc(s("y_sum"), 1)
                after(s("y_copied"), 1, 1)
                after(s("y_added"), 1, -1)
                for q in range(PAIRS):
                    ins = T.transpose(ps[6 + par][:, q * P:(q + 1) * P], t["ysb"][:, q * P:(q + 1) * P], ident)
                ins.then_inc(s("y_turned"), 1)
            if who == "act":
                A = nc.scalar
                for u in range(NU):
                    if u == 7:
                        nxt.exp()
                    e, c = units[u]
                    w = wide_of(u)
                    after(s("up"), NU, u + 1)
                    if layer == 0:
                        A.activation(t["hs"][0:w, u % 2, :], ps[u % 2][0:w, :], ACT.Silu).then_inc(s("act"), 1)
                    else:
                        dst = t["hs"][:, u % 2, :]
                        after(s("gated"), NU, u - 1)
                        A.activation(dst, ps[u % 4][:, :], ACT.Gelu,
                                     bias=t["b1f1"][:, e * CH1 + c:e * CH1 + c + 1]).then_inc(s("act"), 1)
            if who == "dve":
                V = nc.vector
                for u in range(NU):
                    if u == 5:
                        nxt.shifted()
                    if u == 9:
                        nxt.choose()
                    if u == 17:
                        nxt.keep()
                    e, c = units[u]
                    w = wide_of(u)
                    after(s("act"), NU, u + 1)
                    after(s("down"), NU, u - 3)
                    dst = t["hg"][0:w, u % 4, :]
                    if c == 0 and e < E8:
                        hold(eng, S(f"f{layer}_gates{par}"), it * (16 * NG) + 16 * NG) if e == 0 else None
                    if layer == 0:
                        V.tensor_tensor(t["ht"][u % 2][0:w, :], t["hs"][0:w, u % 2, :], ps[2 + u % 2][0:w, :],
                                        ALU.mult).then_inc(s("ht"), 1)
                        after(s("ht"), NU, u + 1)
                        V.tensor_tensor(dst, t["ht"][u % 2][0:w, :], GB[0:w, par, e, :], ALU.mult).then_inc(s("gated"), 1)
                    elif e < E8:
                        V.tensor_tensor(dst, t["hs"][:, u % 2, :], GB[:, par, e, :], ALU.mult).then_inc(s("gated"), 1)
                    else:
                        V.tensor_copy(dst, t["hs"][:, u % 2, :]).then_inc(s("gated"), 1)
                after(s("y_sum"), 1, 1)
                after(s("down"), NU, NU)
                if layer == 0:
                    V.tensor_copy(t["ysb"][:, :], ps[4 + par][:, :]).then_inc(s("y_copied"), 1)
                else:
                    V.tensor_scalar(t["ysb"][:, :], ps[4 + par][:, :], t["b2s"][:, 0:1], None,
                                    ALU.add).then_inc(s("y_copied"), 1)
                after(s("y_turned"), 1, 1)
                xt = X[:, bass.ds(it * (2 * PAIRS) + par * PAIRS, PAIRS), :]
                if layer == 1:
                    after(s("xo_free"), 1, -1)
                xo = t["xo"][:, par, :, :]
                V.tensor_tensor(xo, ps[6 + par][:, :].rearrange("p (q d) -> p q d", q=PAIRS), xt,
                                ALU.add).then_inc(s("y_added"), 1)
                if layer == 0:
                    after(s("y_added"), 1, 1)
                    V.tensor_copy(xt, xo).then_inc(s("x_kept"), 1)
                    after(s("x_kept"), 1, 1)
            if who == "pool" and layer == 1:
                after(s("y_added"), 1, 1)
                eng.dma_start(out[:, bass.ds(it * (2 * PAIRS) + par * PAIRS, PAIRS), :],
                              t["xo"][:, par, :, :]).then_inc(s("stored"), 16)
                after(s("stored"), 16, 16)
                eng.sem_inc(s("xo_free"), 1)


def stage_gnn1_mix(nc, eng, who, S, C, t, ps):
    X = t["X"]
    WAYS = 2
    ND, NP, NA = 12, 3, 4
    ways = range(WAYS)
    dv, pe_s, ac = ([S(f"a1_{n}{w}") for w in ways] for n in ("dve", "pe", "act"))
    xh, ga = (t["xh"], t["gh3"]), (t["ga"], t["gm"])
    banks = [ps[0:3], ps[3:6]]
    with eng.Fori(0, TILES // WAYS) as i:
        def after(sem, per, n):
            hold(eng, sem, i * per + n)

        def x(w):
            return lambda q: X[:, bass.ds(i * (WAYS * PAIRS) + (w * PAIRS + q), 1), :].rearrange("p o d -> p (o d)")

        def tk(w):
            return bass.ds(i * (WAYS * TOK) + w * TOK, TOK)
        if who == "dve":
            V = nc.vector
            for w in ways:
                ln_stats(V, dv[w], t, w, x(w))
            for w in ways:
                after(dv[w], ND, 4)
                ln_sums(V, dv[w], t, w)
            for w in ways:
                after(dv[w], ND, 8)
                ln_var(V, dv[w], t, w)
            for w in ways:
                after(ac[w], NA, 1)
                ln_inverse(V, dv[w], t, w)
            for w in ways:
                after(dv[w], ND, 10)
                ln_apply(V, dv[w], t, w, x(w), xh[w])
            for w in ways:
                after(ac[w], NA, 4)
                for c in range(2):
                    ins = V.bn_stats(t["bnh"][:, c, bass.ds(i * (WAYS * 6) + w * 6, 6)], t["HP"][:, c, tk(w)])
                ins.then_inc(dv[w], 1)
        if who == "pe":
            T = nc.tensor
            for w in ways:
                after(dv[w], ND, 11)
                for q in range(PAIRS):
                    ins = T.matmul(banks[w][0][:, q * P:(q + 1) * P], xh[w][:, q, :], t["AHB"][:, :],
                                   start=True, stop=True)
                ins.then_inc(pe_s[w], 1)
            for w in ways:
                after(ac[w], NA, 2)
                for c in range(2):
                    T.matmul(banks[w][1 + c][:, :], t["w1g1"][:, c * P:(c + 1) * P], ga[w][:, :], start=True,
                             stop=True).then_inc(pe_s[w], 1)
        if who == "act":
            A = nc.scalar
            for w in ways:
                after(dv[w], ND, 9)
                ln_root(A, ac[w], t, w)
            for w in ways:
                after(pe_s[w], NP, 1)
                A.copy(ga[w][:, :], banks[w][0][:, :]).then_inc(ac[w], 1)
            for w in ways:
                for c in range(2):
                    after(pe_s[w], NP, 2 + c)
                    A.activation(t["HP"][:, c, tk(w)], banks[w][1 + c][:, :], ACT.Identity,
                                 bias=t["b1g1"][:, c:c + 1]).then_inc(ac[w], 1)


def batch_norm(nc, eng, who, S, t, n, chunks, stats, gamma, beta, out):
    if who == "dve":
        V = nc.vector
        own = Count(eng, S(f"bn{n}_dve"))
        eng.wait_ge(S(f"bn{n}_stats"), 1)
        for c in range(chunks):
            own.chain(V.bn_aggr(t["bmv"][:, c, :], stats[:, c, :]))
        V.tensor_scalar(t["bsd"][:, 0:chunks], t["bmv"][:, 0:chunks, 1], EPS, None, ALU.add).then_inc(S(f"bn{n}_var"), 1)
        eng.wait_ge(S(f"bn{n}_root"), 1)
        own.chain(V.reciprocal(t["bsd"][:, 4:4 + chunks], t["bsd"][:, 2:2 + chunks]))
        own.chain(V.tensor_tensor(out[:, 0, :], t["bsd"][:, 4:4 + chunks], gamma, ALU.mult))
        own.chain(V.tensor_tensor(t["bsd"][:, 6:6 + chunks], t["bmv"][:, 0:chunks, 0], out[:, 0, :], ALU.mult))
        V.tensor_tensor(out[:, 1, :], beta, t["bsd"][:, 6:6 + chunks], ALU.subtract).then_inc(S(f"bn{n}_ready"), 1)
    if who == "act":
        eng.wait_ge(S(f"bn{n}_var"), 1)
        nc.scalar.activation(t["bsd"][:, 2:2 + chunks], t["bsd"][:, 0:chunks], ACT.Sqrt).then_inc(S(f"bn{n}_root"), 1)


def stage_gnn1_out(nc, eng, who, S, C, t, ps):
    WAYS = 2
    ways = range(WAYS)
    dv, pe_s, ac = ([S(f"b1_{n}{w}") for w in ways] for n in ("dve", "pe", "act"))
    hid = ((t["gh"], t["ga"]), (t["gm"], t["b2row"]))
    with eng.Fori(0, TILES // WAYS) as i:
        def after(sem, per, n):
            hold(eng, sem, i * per + n)

        def tk(w):
            return bass.ds(i * (WAYS * TOK) + w * TOK, TOK)
        if who == "dve":
            for w in ways:
                after(ac[w], 2, 2)
                nc.vector.bn_stats(t["bno"][:, 0, bass.ds(i * (WAYS * 6) + w * 6, 6)], t["xT"][:, tk(w)]
                                   ).then_inc(dv[w], 1)
        if who == "pe":
            for w in ways:
                after(ac[w], 2, 1)
                for c in range(2):
                    ins = nc.tensor.matmul(ps[w][:, :], t["w2g1"][:, c, :], hid[w][c][:, :], start=(c == 0), stop=(c == 1))
                ins.then_inc(pe_s[w], 1)
        if who == "act":
            for w in ways:
                for c, dst in enumerate(hid[w]):
                    ins = nc.scalar.activation(dst[:, :], t["HP"][:, c, tk(w)], ACT.Relu, bias=t["bn1"][:, 1, c:c + 1],
                                               scale=t["bn1"][:, 0, c:c + 1])
                ins.then_inc(ac[w], 1)
            for w in ways:
                after(pe_s[w], 1, 1)
                nc.scalar.activation(t["xT"][:, tk(w)], ps[w][:, :], ACT.Identity,
                                     bias=t["b2g1"][:, 0:1]).then_inc(ac[w], 1)


def stage_gnn1_add(nc, eng, who, S, C, t, ps):
    X, XT = t["X"], t["xT"]
    ident = C[:, C_ID:C_ID + P]
    WAYS = 4
    ND, NP, NA = 13, 2, 2
    ways = range(WAYS)
    dv, pe_s, ac = ([S(f"c1_{n}{w}") for w in ways] for n in ("dve", "pe", "act"))
    xh, gm = t["way"]["xh"], t["way"]["gm"]
    with eng.Fori(0, TILES // WAYS) as i:
        def after(sem, per, n):
            hold(eng, sem, i * per + n)

        def x(w):
            return lambda q: X[:, bass.ds(i * (WAYS * PAIRS) + (w * PAIRS + q), 1), :].rearrange("p o d -> p (o d)")

        def xt(w):
            return X[:, bass.ds(i * (WAYS * PAIRS) + w * PAIRS, PAIRS), :]

        def tk(w):
            return bass.ds(i * (WAYS * TOK) + w * TOK, TOK)
        if who == "dve":
            V = nc.vector
            for w in ways:
                V.tensor_scalar(gm[w][:, :], XT[:, tk(w)], t["bn2"][:, 0, 0:1], t["bn2"][:, 1, 0:1], ALU.mult,
                                ALU.add).then_inc(dv[w], 1)
            for w in ways:
                after(pe_s[w], NP, 1)
                V.tensor_tensor(xt(w), xt(w), pairs(ps[2 * w][:, :]), ALU.add).then_inc(dv[w], 1)
            for w in ways:
                after(dv[w], ND, 2)
                ln_stats(V, dv[w], t, w, x(w))
            for w in ways:
                after(dv[w], ND, 6)
                ln_sums(V, dv[w], t, w)
            for w in ways:
                after(dv[w], ND, 10)
                ln_var(V, dv[w], t, w)
            for w in ways:
                after(ac[w], NA, 1)
                ln_inverse(V, dv[w], t, w)
            for w in ways:
                after(dv[w], ND, 12)
                ln_apply(V, dv[w], t, w, x(w), xh[w])
        if who == "pe":
            T = nc.tensor
            for w in ways:
                after(dv[w], ND, 1)
                for q in range(PAIRS):
                    ins = T.transpose(ps[2 * w][:, q * P:(q + 1) * P], gm[w][:, q * P:(q + 1) * P], ident)
                ins.then_inc(pe_s[w], 1)
            for w in ways:
                after(dv[w], ND, 13)
                for q in range(PAIRS):
                    ins = T.transpose(ps[2 * w + 1][:, q * P:(q + 1) * P], xh[w][:, q, :], ident)
                ins.then_inc(pe_s[w], 1)
        if who == "act":
            for w in ways:
                after(dv[w], ND, 11)
                ln_root(nc.scalar, ac[w], t, w)
            for w in ways:
                after(pe_s[w], NP, 2)
                nc.scalar.copy(XT[:, tk(w)], ps[2 * w + 1][:, :]).then_inc(ac[w], 1)


WREG = 2 * E8 * HID0 + E8 * 3 * P
WREG1 = (E8 + 1) * CH1 * P * 2
HPW = 2 * TILES * TOK


def build(nc, d, out, gates):
    with ExitStack() as ctx:
        def sb(name, shape):
            return ctx.enter_context(nc.sbuf_tensor(name, shape, F32))
        sems = {}

        def S(name):
            if name not in sems:
                sems[name] = ctx.enter_context(nc.semaphore(name))
            return sems[name]
        ps = [ctx.enter_context(nc.psum_tensor(f"bank{i}", [P, 512], F32)) for i in range(8)]
        C = sb("consts", [P, C_COLS])
        hp = sb("hp", [P, HPW])
        wreg = sb("wreg", [P, max(WREG, WREG1)])
        t = dict(gates0=gates[0], gates1=gates[1])
        for name, shape in dict(
            X=[P, N, D], xT=[P, (TILES + 1) * TOK], UB=[P, P], UTB=[P, P], AHB=[P, P],
            w1g0=[P, P], w2g0=[P, P], b1g0=[P, 1], b2row=[P, TOK], wr0=[P, E8], wr1=[P, E8],
            w1g1=[P, 2 * P], b1g1=[P, 2], w2g1=[P, 2, P], b2g1=[P, 1], gb1=[P, 4], gb2=[P, 2],
            b1f1=[P, (E8 + 1) * CH1], b2p=[E8, P], b2s=[P, 1],
            xh=[P, PAIRS, D], gm=[P, TOK], ga=[P, TOK], gh=[P, TOK],
            bn=[P, 4, PAIRS, 6], mv=[P, 4, PAIRS, 2], sd=[P, 4, 12], bnh=[P, 2, TILES * 6], bno=[P, 1, TILES * 6],
            bmv=[P, 2, 2], bsd=[P, 8], bn1=[P, 2, 2], bn2=[P, 2, 1],
            rt=[P, 5, PAIRS * E8], rc=[P, 7, PAIRS], gT=[E8, TOK],
        ).items():
            t[name] = sb(name, shape)
        t["xr"], t["ht"] = t["xh"][:, :, :].rearrange("p q d -> p (q d)"), (t["gm"], t["gh"])
        t["gh3"] = pairs(t["gh"][:, :])
        t["ysb"] = t["ga"]
        t["HP"] = hp[:, :].rearrange("p (c t) -> p c t", c=2)
        t["GB"] = hp[:, 0:2 * E8 * TOK].rearrange("p (b e t) -> p b e t", b=2, e=E8)
        upper = 2 * E8 * TOK

        def part(rows, n, start):
            return hp[0:rows, upper + start * TOK:upper + (start + n) * TOK].rearrange("p (n t) -> p n t", n=n)
        t["g9"], t["hs"], t["hg"] = part(E8, 2, 0), part(P, 2, 2), part(P, 4, 4)
        t["xo"] = hp[:, upper + 8 * TOK:upper + 10 * TOK].rearrange("p (b q d) -> p b q d", b=2, q=PAIRS)
        def ways(k):
            return [hp[:, upper + (4 * k + w) * TOK:upper + (4 * k + w + 1) * TOK] for w in range(4)]
        t["way"] = dict(xh=[pairs(a) for a in ways(0)], ga=ways(1), gh=ways(2), gm=ways(3))
        at = [0]

        def piece(name, shape):
            w = shape[1]
            at[0] += w
            return hp[0:shape[0], at[0] - w:at[0]]
        m = eig_memory(piece, None)
        n1 = E8 * HID0
        t["w1f0"] = wreg[:, 0:n1].rearrange("p (e h) -> p e h", e=E8)
        t["w3f0"] = wreg[:, n1:2 * n1].rearrange("p (e h) -> p e h", e=E8)
        t["w2f0"] = wreg[:, 2 * n1:2 * n1 + E8 * 3 * P].rearrange("p (e c d) -> p e c d", e=E8, c=3)
        half = WREG1 // 2
        t["w1f1"] = wreg[:, 0:half].rearrange("p (e f) -> p e f", e=E8 + 1)
        t["w2f1"] = wreg[:, half:2 * half].rearrange("p (e c d) -> p e c d", e=E8 + 1, c=CH1)
        block = ctx.enter_context(nc.Block())

        def program(eng, who):
            if who == "dve":
                eig_vector(nc, eng, S, C, m, ps, 0, 0, t["UB"], t["UTB"], t["AHB"])
                eng.wait_ge(S("x_in"), 32)
                eng.wait_ge(S("small_in"), SMALL)
            if who == "pe":
                eig_tensor(nc, eng, S, C, m, ps)
                eng.wait_ge(S("small_in"), SMALL)
            if who == "act":
                eig_scalar(nc, eng, S, m, ps)
                eng.wait_ge(S("small_in"), SMALL)
            stage_gnn0(nc, eng, who, S, C, t, ps)
            if who == "pe":
                eng.wait_ge(S("w0_in"), W0)
            if who == "pool":
                nc.gpsimd.memset(t["xT"][:, TILES * TOK:(TILES + 1) * TOK], 0.0).then_inc(S("pad_zero"), 1)
                eng.wait_ge(S("pad_zero"), 1)
            if who in ("pe", "pool", "dve"):
                for w in range(4):
                    eng.wait_ge(S(f"g0_act{w}"), 5 * TILES // 4)
            stage_experts(nc, eng, who, S, C, t, ps, 0)
            if who == "sp":
                eng.wait_ge(S("f0_gates0"), 16 * E8 * (TILES // 2 + 1))
                eng.wait_ge(S("f0_gates1"), 16 * E8 * TILES // 2)
                eng.wait_ge(S("f0_down"), E8 * 3 * (TILES + 1) + 1)
                half = (E8 + 1) * CH1 * P
                eng.dma_start(t["w1f1"][:, 0:E8, :], d["w1p"]).then_inc(S("w1_in"), 16)
                eng.dma_start(t["w1f1"][:, E8, :], d["w1s"]).then_inc(S("w1_in"), 16)
                for e in range(E8):
                    eng.dma_start(t["w2f1"][:, e, :, :], d["w2p"][e].rearrange("(c f) d -> f c d", f=P)
                                  ).then_inc(S("w1_in"), 16)
                eng.dma_start(t["w2f1"][:, E8, :, :], d["w2s"].rearrange("(c f) d -> f c d", f=P)
                              ).then_inc(S("w1_in"), 16)
            if who == "act":
                eng.wait_ge(S("f0_gates0"), 16 * E8 * (TILES // 2 + 1))
                eng.wait_ge(S("f0_y_added"), TILES + E8 * 3 + 1)
                eng.wait_ge(S("r0_dve"), Route.ND * (TILES + 1))
            stage_gnn1_mix(nc, eng, who, S, C, t, ps)
            if who == "dve":
                for w in range(2):
                    eng.wait_ge(S(f"a1_dve{w}"), 12 * TILES // 2)
                eng.nop().then_inc(S("bn1_stats"), 1)
            batch_norm(nc, eng, who, S, t, 1, 2, t["bnh"], t["gb1"][:, 0:2], t["gb1"][:, 2:4], t["bn1"])
            if who == "act":
                eng.wait_ge(S("bn1_ready"), 1)
            stage_gnn1_out(nc, eng, who, S, C, t, ps)
            if who == "dve":
                for w in range(2):
                    eng.wait_ge(S(f"b1_dve{w}"), TILES // 2)
                eng.nop().then_inc(S("bn2_stats"), 1)
            batch_norm(nc, eng, who, S, t, 2, 1, t["bno"], t["gb2"][:, 0:1], t["gb2"][:, 1:2], t["bn2"])
            if who == "dve":
                eng.wait_ge(S("bn2_ready"), 1)
            stage_gnn1_add(nc, eng, who, S, C, t, ps)
            if who == "pe":
                eng.wait_ge(S("w1_in"), 16 * (E8 + 3))
            if who in ("pe", "pool", "dve", "sp"):
                for w in range(4):
                    eng.wait_ge(S(f"c1_act{w}"), 2 * TILES // 4)
            stage_experts(nc, eng, who, S, C, t, ps, 1, out)
            if who == "sp":
                eng.wait_ge(S("f1_gates0"), 16 * (E8 + 1) * (TILES // 2 + 1))
            if who == "pool":
                eng.wait_ge(S("f1_stored"), 16 * TILES)

        small = [
            (t["w1g0"][:, :], d["w1g0"]), (t["w2g0"][:, :], d["w2g0"]), (t["b1g0"][:, :], d["b1g0"]),
            *[(t["b2row"][:, q * P:(q + 1) * P], d["b2g0"].to_broadcast([P, P])) for q in range(PAIRS)],
            (t["wr0"][:, :], d["wr0"]), (t["wr1"][:, :], d["wr1"]), (t["w1g1"][:, :], d["w1g1"]),
            (t["b1g1"][:, :], d["b1g1"]), (t["w2g1"][:, :, :], d["w2g1"].rearrange("(c f) d -> f c d", f=P)),
            (t["b2g1"][:, :], d["b2g1"]),
            (t["gb1"][:, 0:2], d["g1"]), (t["gb1"][:, 2:4], d["be1"]), (t["gb2"][:, 0:1], d["g2"]),
            (t["gb2"][:, 1:2], d["be2"]), (t["b1f1"][:, 0:E8 * CH1], d["b1p"]),
            (t["b1f1"][:, E8 * CH1:], d["b1s"]), (t["b2p"][:, :], d["b2p"]), (t["b2s"][:, :], d["b2s"]),
        ]
        SMALL = 16 * len(small)
        W0 = 16 * 5

        @block.sync
        def _(sp):
            sp.dma_start(C[:, :], d["consts"]).then_inc(S("const_in"), 16)
            sp.dma_start(m["A"], d["adj"]).then_inc(S("adj_in"), 16)
            sp.dma_start(m["AT"][0:N, :], d["adjT"]).then_inc(S("adj_in"), 16)
            sp.dma_start(m["AT"][N:P, :], d["adjT"]).then_inc(S("adj_in"), 16)
            for h in range(2):
                sp.dma_start(t["X"][h * N:(h + 1) * N, :, :],
                             d["x"].rearrange("(p two) n d -> two n p d", two=2)[h]).then_inc(S("x_in"), 16)
            for dst, src in small:
                sp.dma_start(dst, src).then_inc(S("small_in"), 16)
            sp.dma_start(t["w1f0"], d["w1f0"]).then_inc(S("w0_in"), 16)
            sp.dma_start(t["w3f0"], d["w3f0"]).then_inc(S("w0_in"), 16)
            for c, (a, w) in enumerate(CH0):
                sp.dma_start(t["w2f0"][0:w, :, c, :], d["w2f0"][a:a + w]).then_inc(S("w0_in"), 16)
            program(sp, "sp")

        @block.tensor
        def _(pe):
            program(pe, "pe")

        @block.vector
        def _(dve):
            program(dve, "dve")

        @block.scalar
        def _(act):
            program(act, "act")

        @block.gpsimd
        def _(pool):
            program(pool, "pool")


def kernel(x, adj, L0_gnn_W1, L0_gnn_b1, L0_gnn_W2, L0_gnn_b2, L0_ffn_router_w, L0_ffn_w1, L0_ffn_w2, L0_ffn_w3,
           L1_gnn_W1, L1_gnn_b1, L1_gnn_g1, L1_gnn_be1, L1_gnn_W2, L1_gnn_b2, L1_gnn_g2, L1_gnn_be2,
           L1_ffn_Wr, L1_ffn_W1s, L1_ffn_b1s, L1_ffn_W2s, L1_ffn_b2s, L1_ffn_W1p, L1_ffn_b1p, L1_ffn_W2p, L1_ffn_b2p):
    import concourse.bacc as bacc
    from concourse.bass_utils import run_bass_kernel_spmd
    A = np.asarray

    def column(a, n=1):
        return A(a).reshape(n, P).T
    arrays = dict(
        consts=constants(), x=A(x), adj=A(adj), adjT=A(adj).T,
        w1g0=A(L0_gnn_W1), b1g0=column(L0_gnn_b1), w2g0=A(L0_gnn_W2), b2g0=A(L0_gnn_b2).reshape(1, P),
        wr0=A(L0_ffn_router_w).T, w1f0=A(L0_ffn_w1).transpose(2, 0, 1), w3f0=A(L0_ffn_w3).transpose(2, 0, 1),
        w2f0=A(L0_ffn_w2).transpose(2, 0, 1),
        w1g1=A(L1_gnn_W1).T, b1g1=column(L1_gnn_b1, 2), g1=column(L1_gnn_g1, 2), be1=column(L1_gnn_be1, 2),
        w2g1=A(L1_gnn_W2).T, b2g1=column(L1_gnn_b2), g2=column(L1_gnn_g2), be2=column(L1_gnn_be2),
        wr1=A(L1_ffn_Wr), w1s=A(L1_ffn_W1s), b1s=column(L1_ffn_b1s, CH1), w2s=A(L1_ffn_W2s), b2s=column(L1_ffn_b2s),
        w1p=A(L1_ffn_W1p).transpose(1, 0, 2), b1p=column(L1_ffn_b1p, E8 * CH1), w2p=A(L1_ffn_W2p), b2p=A(L1_ffn_b2p),
    )
    arrays = {f"in_{k}": np.ascontiguousarray(v) for k, v in arrays.items()}
    nc = bacc.Bacc("TRN2", target_bir_lowering=False, num_devices=1)
    d = {k[3:]: nc.dram_tensor(k, v.shape, F32, kind="ExternalInput").ap() for k, v in arrays.items()}
    out = nc.dram_tensor("out", (N, P, D), F32, kind="ExternalOutput").ap()
    gates = [nc.dram_tensor(f"gates{n}", (E8, (TILES + 1) * TOK), F32).ap() for n in range(2)]
    build(nc, d, out.rearrange("q r d -> r q d"), gates)
    r = run_bass_kernel_spmd(nc, [arrays], core_ids=[0])
    return r.results[0]["out"].reshape(2 * N, N, D)
```
